# Optimizing a Trainium2 kernel written in Bass

```python
import numpy as np
import jax
import jax.numpy as jnp

def _softmax(x, axis=-1):
    return jax.nn.softmax(x, axis=axis)

def _gelu(x):
    return jax.nn.gelu(x, approximate=True)

def _silu(x):
    return jax.nn.silu(x)

def _sigmoid(x):
    return jax.nn.sigmoid(x)

def _layernorm(x, axis=-1, eps=1e-05):
    m = jnp.mean(x, axis=axis, keepdims=True)
    v = jnp.var(x, axis=axis, keepdims=True)
    return (x - m) / jnp.sqrt(v + eps)

def _scatter_add(tgt, idx, src, axis=0):
    return tgt.at[idx].add(src)

def _segment_sum(src, seg, n):
    return jax.ops.segment_sum(src, seg, n)
kernel_name = 'mk_xattn_ffn_d1_seqx_r2_37fffd'

def setup_inputs(seed: int=0):
    np.random.seed(seed)
    _w = jnp.asarray

    def _rec_inputs():
        import jax
        import jax.numpy as jnp
        _rk = jax.random.key(seed)
        x = -0.0002928 + 1 * jax.random.normal(jax.random.fold_in(_rk, 1), (4, 2048, 512), jnp.float32)
        _lenS = 2048 - jax.random.randint(jax.random.fold_in(_rk, 7), (4,), 0, max(1, 2048 // 4) + 1, jnp.int32)
        _lenS2 = 77 - jax.random.randint(jax.random.fold_in(_rk, 8), (4,), 0, max(1, 77 // 4) + 1, jnp.int32)
        _ctx_1024P = jax.random.normal(jax.random.fold_in(_rk, 11), (4, 16, 512), jnp.float32)
        _ctx_1024c = jax.random.dirichlet(jax.random.fold_in(_rk, 511), 0.3 * jnp.ones((16,), jnp.float32), (4, 77))
        _ctx_1024t = jnp.einsum('bsk,bkd->bsd', _ctx_1024c, _ctx_1024P)
        _ctx_1024t = _ctx_1024t * jax.lax.rsqrt(jnp.mean(jnp.square(_ctx_1024t)) + 1e-12) * 0.953939
        ctx_1024 = -1.39393e-06 + 0.999914 * (_ctx_1024t + 0.3 * jax.random.normal(jax.random.fold_in(_rk, 611), (4, 77, 512), jnp.float32))
        _validS = jnp.arange(2048)[None, :] < _lenS[:, None]
        _validS2 = jnp.arange(77)[None, :] < _lenS2[:, None]
        _causal = jnp.tril(jnp.ones((2048, 2048), dtype=bool))
        mask_1x1xSxS2_ik0 = jnp.where(jnp.broadcast_to(_validS2[0:1, None, None, :], (1, 1, 2048, 77)), 0, 1).astype(jnp.int32)
        return (x, ctx_1024, mask_1x1xSxS2_ik0)
    x, ctx_1024, mask_1x1xSxS2_ik0 = _rec_inputs()

    def _L0_xattn_setup():
        import jax, jax.numpy as jnp
        import numpy as np
        D_MODEL = 512
        HEADS = 16
        D_K = D_MODEL // HEADS
        B, S = (2, 1024)
        key = jax.random.key(seed)
        k1, k2, k3, k4, k5, k6, k7 = jax.random.split(key, 7)
        scale = 1.0 / np.sqrt(D_MODEL)
        inp = {'q_src': jax.random.normal(k1, (B, S, D_MODEL), jnp.float32), 'k_src': jax.random.normal(k2, (B, S, D_MODEL), jnp.float32), 'v_src': jax.random.normal(k3, (B, S, D_MODEL), jnp.float32), 'mask': jnp.tril(jnp.ones((S, S), jnp.int32))[None, None], 'Wq': jax.random.normal(k4, (D_MODEL, D_MODEL), jnp.float32) * scale, 'Wk': jax.random.normal(k5, (D_MODEL, D_MODEL), jnp.float32) * scale, 'Wv': jax.random.normal(k6, (D_MODEL, D_MODEL), jnp.float32) * scale, 'Wo': jax.random.normal(k7, (D_MODEL, D_MODEL), jnp.float32) * scale}
        return inp
    _L0_xattn_all = _L0_xattn_setup()
    _L0_xattn_in = {k: v for k, v in _L0_xattn_all.items() if k in ('Wq', 'Wk', 'Wv', 'Wo')}
    del _L0_xattn_all

    def _L0_ffn_setup():
        import jax, jax.numpy as jnp
        import numpy as np
        D_MODEL = 512
        M = 64
        INNER = 16
        key = jax.random.key(seed)
        ks = jax.random.split(key, 9)

        def init(k, shape, fan_in):
            bound = 1.0 / np.sqrt(fan_in)
            return jax.random.uniform(k, shape, jnp.float32, -bound, bound)
        x = jax.random.normal(ks[0], (16, 2048, D_MODEL), dtype=jnp.float32)
        Win = init(ks[1], (D_MODEL, M), D_MODEL)
        bin_ = init(ks[2], (M,), D_MODEL)
        W1 = init(ks[3], (M, INNER), 1)
        b1 = init(ks[4], (M, INNER), 1)
        W2 = init(ks[5], (M, INNER), INNER)
        b2 = init(ks[6], (M,), INNER)
        Wout = init(ks[7], (M, D_MODEL), M)
        bout = init(ks[8], (D_MODEL,), M)
        return {'x': x, 'Win': Win, 'bin_': bin_, 'W1': W1, 'b1': b1, 'W2': W2, 'b2': b2, 'Wout': Wout, 'bout': bout}
    _L0_ffn_all = _L0_ffn_setup()
    _L0_ffn_in = {k: v for k, v in _L0_ffn_all.items() if k in ('Win', 'bin_', 'W1', 'b1', 'W2', 'b2', 'Wout', 'bout')}
    del _L0_ffn_all
    return {'x': x, 'ctx_1024': ctx_1024, 'mask_1x1xSxS2_ik0': mask_1x1xSxS2_ik0, 'L0_xattn_Wq': _L0_xattn_in['Wq'], 'L0_xattn_Wk': _L0_xattn_in['Wk'], 'L0_xattn_Wv': _L0_xattn_in['Wv'], 'L0_xattn_Wo': _L0_xattn_in['Wo'], 'L0_ffn_Win': _L0_ffn_in['Win'], 'L0_ffn_bin_': _L0_ffn_in['bin_'], 'L0_ffn_W1': _L0_ffn_in['W1'], 'L0_ffn_b1': _L0_ffn_in['b1'], 'L0_ffn_W2': _L0_ffn_in['W2'], 'L0_ffn_b2': _L0_ffn_in['b2'], 'L0_ffn_Wout': _L0_ffn_in['Wout'], 'L0_ffn_bout': _L0_ffn_in['bout']}

def reference(x, ctx_1024, mask_1x1xSxS2_ik0, L0_xattn_Wq, L0_xattn_Wk, L0_xattn_Wv, L0_xattn_Wo, L0_ffn_Win, L0_ffn_bin_, L0_ffn_W1, L0_ffn_b1, L0_ffn_W2, L0_ffn_b2, L0_ffn_Wout, L0_ffn_bout):
    import jax
    import jax.numpy as jnp

    def _L0_xattn_ref(q_src, k_src, v_src, mask, Wq, Wk, Wv, Wo):
        import jax, jax.numpy as jnp
        import numpy as np
        D_MODEL = 512
        HEADS = 16
        D_K = D_MODEL // HEADS
        B, S = (2, 1024)
        q = q_src @ Wq.T
        k = k_src @ Wk.T
        v = v_src @ Wv.T

        def split_heads(x):
            b, s, _ = x.shape
            return x.reshape(b, s, HEADS, D_K).transpose(0, 2, 1, 3)
        q, k, v = (split_heads(q), split_heads(k), split_heads(v))
        logits = jnp.einsum('bhqd,bhkd->bhqk', q, k) / np.sqrt(D_K)
        logits = jnp.where(mask == 0, jnp.float32(-1000000000.0), logits)
        probs = jax.nn.softmax(logits, axis=-1)
        a = jnp.einsum('bhqk,bhkd->bhqd', probs, v)
        a = a.transpose(0, 2, 1, 3).reshape(q_src.shape[0], -1, D_MODEL)
        return a @ Wo.T

    def _L0_ffn_ref(x, Win, bin_, W1, b1, W2, b2, Wout, bout):
        import jax, jax.numpy as jnp
        import numpy as np
        D_MODEL = 512
        M = 64
        INNER = 16
        s = jnp.einsum('btd,dm->btm', x, Win) + bin_
        h = jax.nn.relu(s[..., None] * W1 + b1)
        g = jnp.einsum('btmh,mh->btm', h, W2) + b2
        out = jnp.einsum('btm,md->btd', g, Wout) + bout
        return out
    x = x + _L0_xattn_ref(_layernorm(x, axis=-1), ctx_1024, ctx_1024, mask_1x1xSxS2_ik0, L0_xattn_Wq, L0_xattn_Wk, L0_xattn_Wv, L0_xattn_Wo)
    x = x + _L0_ffn_ref(_layernorm(x, axis=-1), L0_ffn_Win, L0_ffn_bin_, L0_ffn_W1, L0_ffn_b1, L0_ffn_W2, L0_ffn_b2, L0_ffn_Wout, L0_ffn_bout)
    return x

_drawn_inputs = setup_inputs


def setup_inputs(seed=0):
    import zlib

    import numpy as np

    out = dict(_drawn_inputs(seed))
    spreads = {}
    factors = {'L0_ffn_bin_': 24.977}
    for name, (base, spread) in spreads.items():
        noise = np.random.default_rng([zlib.crc32(name.encode()), seed]).standard_normal(out[name].shape)
        drawn = base * np.exp(spread * noise) if base else spread * noise
        out[name] = jnp.asarray(drawn.astype(out[name].dtype))
    for name, factor in factors.items():
        out[name] = (out[name] * factor).astype(out[name].dtype)
    return out
```

```python
from contextlib import ExitStack

import concourse.bass as bass
from concourse import mybir

F32 = mybir.dt.float32
F16 = mybir.dt.float16
BF16 = mybir.dt.bfloat16
I32 = mybir.dt.int32
ALU = mybir.AluOpType
ACT = mybir.ActivationFunctionType
AX = mybir.AxisListType

P = 128
D = 512
C = D // P
B = 4
S = 2048
T = 4
ROWS = T * P
GROUPS = B * S // ROWS
PER_BATCH = GROUPS // B
KEYS = 77
HEADS = 16
DK = D // HEADS
HC = P // DK
LW = HC * KEYS
HALVES = 2 * T
M = 64
INNER = 16
J = M * INNER // P
MJ = M // J
W_SCALE = 16.0
MASKED = -(2.0 ** 100)
EPS = 1e-5

SETUP, FRONT, SOFT, BACK = "setup", "front", "soft", "back"

TR_SETUP = [("ctxT", c) for c in range(C)] + [(w, c) for w in ("wk", "wv", "wq", "wo") for c in range(C)]
TR_ORDER = (
    [(BACK, "pT", h) for h in range(HEADS)]
    + [(FRONT, "xT", t) for t in range(T)]
    + [(BACK, "hT", t) for t in range(T)]
    + [(BACK, "pre", j) for j in range(J)]
)
MM_SETUP = [("k", c) for c in range(C)] + [("v", b) for b in range(B)]
MM_ORDER = (
    [(BACK, "pv", c) for c in range(C)]
    + [(BACK, "wo", t) for t in range(T)]
    + [(FRONT, "q", 0), (FRONT, "q", 1), (FRONT, "q", 2), (BACK, "s", 0), (FRONT, "q", 3), (BACK, "g", 0)]
    + [(BACK, "out", t) for t in range(T)]
)


class Step:

    def __init__(self, t, v, parts=(FRONT, SOFT, BACK)):
        self.t, self.v, self.parts = t, v, parts
        self.i = 4 * t + v

    def group(self, ahead):
        return Group(self.t, self.v + ahead)


class Group:

    def __init__(self, t, v):
        self.n, self.slot, self.lap, self.parity = 4 * t + v, v % 4, t + v // 4, v % 2


class Ring:

    def __init__(self, setup, order, tensor, ready, free):
        self.setup, self.order, self.tensor, self.ready, self.free = setup, order, tensor, ready, free
        self.fronts = sum(part == FRONT for part, _, _ in order)

    def half(self, step):
        before = len(self.setup)
        if step is SETUP:
            return 0
        if isinstance(step.i, int) and step.i < 1:
            return (before + self.fronts * (step.i + 1)) // 2
        half = (before + 2 * self.fronts) // 2 + (step.i - 1) * (len(self.order) // 2)
        if isinstance(step.i, int) and step.i == GROUPS:
            half -= self.fronts // 2
        return half

    def place(self, step, name, k):
        if step is SETUP:
            return self.setup.index((name, k))
        return [(n, m) for part, n, m in self.order if part in step.parts].index((name, k))

    def bank(self, step, name, k):
        return self.tensor[:, self.place(step, name, k) % 2, :]

    def wait_free(self, eng, step, name, k):
        place = self.place(step, name, k)
        value = self.half(step) + place // 2
        if not (isinstance(value, int) and value < 1):
            eng.wait_ge(self.free[place % 2], value)

    def wait_ready(self, eng, step, name, k):
        eng.wait_ge(self.ready, 2 * self.half(step) + self.place(step, name, k) + 1)

    def wait_read(self, eng, step, name, k):
        place = self.place(step, name, k)
        eng.wait_ge(self.free[place % 2], self.half(step) + place // 2 + 1)

    def read(self, instruction, step, name, k):
        instruction.then_inc(self.free[self.place(step, name, k) % 2], 1)


def build(nc, x, ctx_in, mask, Wq, Wk, Wv, Wo, Win, bin_, W1, b1, W2, b2, Wout, bout, out):
    stack = ExitStack()
    with stack:
        def sb(name, shape, dt):
            return stack.enter_context(nc.sbuf_tensor(name, shape, dt))

        def sem(name):
            return stack.enter_context(nc.semaphore(name))

        tr_banks = stack.enter_context(nc.psum_tensor("tr_banks", [P, 2, D], F32))
        mm_banks = stack.enter_context(nc.psum_tensor("mm_banks", [P, 2, D], F32))
        lg_banks = stack.enter_context(nc.psum_tensor("lg_banks", [P, 2, 2, 512], F32))

        ident = sb("ident", [P, P], F32)
        ident_bf = sb("ident_bf", [P, P], BF16)
        wqT = sb("wqT", [P, 2, C, D], F16)
        woT = sb("woT", [P, 2, C, D], F16)
        win_f = sb("win_f", [P, C, 2, M], F32)
        win = sb("win", [P, 2, C, 2 * M], F16)
        kT_all = sb("kT_all", [P, B, 2, C, KEYS], F16)
        k_blocks = sb("k_blocks", [P, 2, C, LW], F16)
        v_all = sb("v_all", [KEYS, B, D], F32)
        v_now = sb("v_now", [KEYS, D], F32)
        mask_bias = sb("mask_bias", [P, PER_BATCH, T, KEYS], BF16)
        spread = sb("spread", [P, J, P], F16)
        w1_col = sb("w1_col", [P, J], F32)
        w1_div = sb("w1_div", [P, J], F32)
        b1_col = sb("b1_col", [P, J], F32)
        w2_col = sb("w2_col", [P, J], F32)
        units = sb("units", [P, MJ], F32)
        w2_blocks = sb("w2_blocks", [P, J, DK], F32)
        bin_col = sb("bin_col", [P, 1], F32)
        bin16 = sb("bin16", [P, 1], F32)
        b2_col = sb("b2_col", [P, 1], F32)
        wout = sb("wout", [P, D], F32)
        neg_half = sb("neg_half", [P, T], F32)

        xr = sb("xr", [P, 4, T, D], F32)
        xn = sb("xn", [P, T, D], F32)
        hn = sb("hn", [P, T, D], F32)
        xT = sb("xT", [P, 2, C, ROWS], F16)
        hT = sb("hT", [P, 2, C, ROWS], F16)
        qT = sb("qT", [P, 2, 2, C, ROWS], F16)
        probs = sb("probs", [P, 2, T, HEADS * KEYS], F32)
        pT = sb("pT", [P, 8, ROWS], F32)
        aT = sb("aT", [P, 2, C, ROWS], F16)
        s_parts = sb("s_parts", [P, ROWS], F16)
        inner = sb("inner", [P, 4, ROWS], F32)
        gT = sb("gT", [P, ROWS], F32)
        stats = sb("stats", [P, 2, T, 6], F32)
        mean_var = sb("mean_var", [P, 2, T, 2], F32)
        var_eps = sb("var_eps", [P, 2, T], F32)
        rstd = sb("rstd", [P, 2, T], F32)
        row_max = sb("row_max", [P, 2, 2, HC], F32)
        row_sum = sb("row_sum", [P, 2, 2, HC], F32)
        row_inv = sb("row_inv", [P, 2, HALVES, 2, HC], F32)

        w_raw = probs[:, :, :, :].rearrange("p a t n -> p (a t n)")[:, 0:4 * C * D].rearrange(
            "p (w c n) -> p w c n", w=4, c=C)
        wkT = pT[:, 0:4, :]
        wvT = pT[:, 4:8, :]
        ctxT = xr[:, 2, :, 0:B * KEYS]
        ctx_raw = xr[0:KEYS, 3, :, :]
        mask_raw = hn[:, :, 0:T * KEYS].bitcast(I32)

        ctx_loaded = sem("ctx_loaded")
        w_loaded = [sem(f"w_loaded_{w}") for w in ("k", "v", "q", "o")]
        mask_loaded = sem("mask_loaded")
        ffn_loaded = sem("ffn_loaded")
        x_loaded = [sem(f"x_loaded_{s}") for s in range(4)]
        out_stored = [sem(f"out_stored_{s}") for s in range(4)]
        pool_const = sem("pool_const")
        ffn_const = sem("ffn_const")
        mask_ready = sem("mask_ready")
        zeroed = sem("zeroed")
        tr_ready = sem("tr_ready")
        mm_ready = sem("mm_ready")
        lg_ready = sem("lg_ready")
        tr_free = [sem("tr_free_0"), sem("tr_free_1")]
        mm_free = [sem("mm_free_0"), sem("mm_free_1")]
        lg_free = sem("lg_free")
        setup_high = sem("setup_high")
        win_high = sem("win_high")
        x_stats = sem("x_stats")
        x_mean = sem("x_mean")
        x_eps = sem("x_eps")
        x_rstd = sem("x_rstd")
        x_norm = sem("x_norm")
        x_high = sem("x_high")
        q_high = sem("q_high")
        max_done = sem("max_done")
        exp_done = sem("exp_done")
        sum_done = sem("sum_done")
        inv_done = sem("inv_done")
        probs_ready = sem("probs_ready")
        k_ready = sem("k_ready")
        v_ready = sem("v_ready")
        a_high = sem("a_high")
        h_stats = sem("h_stats")
        h_mean = sem("h_mean")
        h_eps = sem("h_eps")
        h_rstd = sem("h_rstd")
        h_norm = sem("h_norm")
        h_high = sem("h_high")
        s_high = sem("s_high")

        tr = Ring(TR_SETUP, TR_ORDER, tr_banks, tr_ready, tr_free)
        mm = Ring(MM_SETUP, MM_ORDER, mm_banks, mm_ready, mm_free)

        x_rows = x.rearrange("b (g p t) d -> (b g) p t d", p=P, t=T)
        out_rows = out.rearrange("b (g p t) d -> (b g) p t d", p=P, t=T)

        def run(eng, one_step):
            one_step(Step(0, -1, (FRONT,)))
            one_step(Step(0, 0, (FRONT, SOFT)))
            with eng.Fori(0, GROUPS // 4 - 1, 1) as t:
                for v in range(1, 5):
                    one_step(Step(t, v))
            for v in range(GROUPS - 3, GROUPS - 1):
                one_step(Step(0, v))
            one_step(Step(0, GROUPS - 1, (SOFT, BACK)))
            one_step(Step(0, GROUPS, (BACK,)))

        block = stack.enter_context(nc.Block())

        @block.sync
        def _(sp):
            sp.dma_start(ctx_raw, ctx_in.rearrange("b k d -> k b d")).then_inc(ctx_loaded, 16)
            for n, w in enumerate((Wk, Wv, Wq, Wo)):
                sp.dma_start(w_raw[:, n, :, :], w.rearrange("(c p) n -> p c n", p=P)).then_inc(w_loaded[n], 16)
            for n in range(2):
                sp.dma_start(xr[:, n, :, :], x_rows[n]).then_inc(x_loaded[n], 16)
            mm.wait_ready(sp, SETUP, "v", B - 1)
            for n in range(2, 4):
                sp.dma_start(xr[:, n, :, :], x_rows[n]).then_inc(x_loaded[n], 16)

            def store(step):
                g = step.group(-1)
                mm.wait_read(sp, step, "out", T - 2)
                mm.wait_read(sp, step, "out", T - 1)
                sp.dma_start(out_rows[g.n], xr[:, g.slot, :, :]).then_inc(out_stored[g.slot], 16)

            def load(step):
                g = step.group(3)
                sp.wait_ge(out_stored[g.slot], 16 * g.lap)
                sp.dma_start(xr[:, g.slot, :, :], x_rows[g.n]).then_inc(x_loaded[g.slot], 16)

            with sp.Fori(0, GROUPS // 4 - 1, 1) as t:
                for v in range(1, 5):
                    store(Step(t, v))
                    load(Step(t, v))
            for v in range(GROUPS - 3, GROUPS - 1):
                store(Step(0, v))
            store(Step(0, GROUPS - 1, (SOFT, BACK)))
            store(Step(0, GROUPS, (BACK,)))
            for s in range(4):
                sp.wait_ge(out_stored[s], 16 * (GROUPS // 4))

        @block.gpsimd
        def _(pool):
            pool.memset(ident[:, :], 0.0).then_inc(pool_const, 1)
            pool.memset(ident_bf[:, :], 0.0).then_inc(pool_const, 1)
            pool.wait_ge(pool_const, 2)
            for m in (ident, ident_bf):
                pool.affine_select(out=m[:, :], in_=m[:, :], compare_op=ALU.not_equal, fill=1.0, base=0,
                                   pattern=[[-1, P]], channel_multiplier=1).then_inc(pool_const, 1)
            pool.memset(neg_half[:, :], -0.5).then_inc(pool_const, 1)
            pool.memset(k_blocks[:, :, :, :], 0.0).then_inc(pool_const, 1)
            pool.memset(spread[:, :, :], 0.0).then_inc(pool_const, 1)
            pool.memset(units[:, :], 1.0).then_inc(pool_const, 1)
            for n, first in enumerate((0, -M)):
                pool.wait_ge(pool_const, 8 + n)
                v = spread[:, :, :].rearrange("p j (i n) -> p j i n", n=INNER)
                pool.affine_select(out=v, in_=v, compare_op=ALU.not_equal, fill=1.0, base=first,
                                   pattern=[[-MJ, J], [-1, MJ], [0, INNER]], channel_multiplier=1)\
                    .then_inc(pool_const, 1)
            pool.wait_ge(pool_const, 10)
            pool.affine_select(out=units[:, :], in_=units[:, :], compare_op=ALU.is_ge, fill=0.0, base=0,
                               pattern=[[-INNER, MJ]], channel_multiplier=1).then_inc(pool_const, 1)
            pool.wait_ge(pool_const, 11)
            pool.affine_select(out=units[:, :], in_=units[:, :], compare_op=ALU.is_ge, fill=0.0, base=INNER - 1,
                               pattern=[[INNER, MJ]], channel_multiplier=-1).then_inc(pool_const, 1)

            def front(step):
                n = step.i + 1
                pool.wait_ge(x_eps, n + 1)
                pool.tensor_tensor(rstd[:, 0, :], var_eps[:, 0, :], neg_half[:, :], ALU.pow).then_inc(x_rstd, 1)

            def back_rstd(step):
                n = step.i - 1
                pool.wait_ge(h_eps, n + 1)
                pool.tensor_tensor(rstd[:, 1, :], var_eps[:, 1, :], neg_half[:, :], ALU.pow).then_inc(h_rstd, 1)

            def divide(step, k):
                n = HALVES * step.i + k
                g = step.group(0)
                t, u = k // 2, k % 2
                pool.wait_ge(inv_done, n + 1)
                p = probs[:, g.parity, t, 8 * KEYS * u:8 * KEYS * (u + 1)].rearrange("p (b h k) -> p b h k", b=2, h=HC)
                inv = row_inv[:, g.parity, k, :, :].unsqueeze(3).broadcast_to([P, 2, HC, KEYS])
                pool.tensor_tensor(p, p, inv, ALU.mult).then_inc(probs_ready, 1)

            def one_step(step):
                if FRONT in step.parts:
                    front(step)
                if SOFT in step.parts:
                    for k in range(5):
                        divide(step, k)
                if BACK in step.parts:
                    back_rstd(step)
                if SOFT in step.parts:
                    for k in range(5, HALVES):
                        divide(step, k)

            run(pool, one_step)

        @block.scalar
        def _(act):
            act.dma_start(mask_raw, mask[0, 0].rearrange("(g p t) k -> p g (t k)", p=P, t=T)).then_inc(mask_loaded, 16)
            for twice in range(2):
                act.dma_start(win_f[:, :, twice, :], Win.rearrange("(c p) m -> p c m", p=P)).then_inc(ffn_loaded, 16)
                act.dma_start(bin_col[M * twice:M * (twice + 1), :], bin_.rearrange("(m a) -> m a", a=1))\
                    .then_inc(ffn_loaded, 16)
            for col, w in ((w1_col, W1), (b1_col, b1), (w2_col, W2)):
                act.dma_start(col[:, :], w.rearrange("(j i) n -> (i n) j", i=MJ), allow_slow_non_contiguous=True)\
                    .then_inc(ffn_loaded, 16)
            act.wait_ge(ffn_const, 2)
            for j in range(J):
                first = DK * (j % 4) + MJ * (j // 4)
                act.dma_start(wout[first:first + MJ, :], Wout[MJ * j:MJ * (j + 1), :]).then_inc(ffn_loaded, 16)
                act.dma_start(b2_col[first:first + MJ, :], b2[MJ * j:MJ * (j + 1)].rearrange("(m a) -> m a", a=1))\
                    .then_inc(ffn_loaded, 16)
            act.dma_start(wout[2 * MJ:2 * MJ + 1, :], bout.rearrange("(a d) -> a d", a=1)).then_inc(ffn_loaded, 16)

            for c in range(C):
                tr.wait_ready(act, SETUP, "ctxT", c)
                tr.read(act.activation(ctxT[:, c, :], tr.bank(SETUP, "ctxT", c)[:, 0:B * KEYS], ACT.Copy),
                        SETUP, "ctxT", c)
            for c in range(C):
                tr.wait_ready(act, SETUP, "wk", c)
                tr.read(act.activation(wkT[:, c, :], tr.bank(SETUP, "wk", c), ACT.Copy), SETUP, "wk", c)
            for c in range(C):
                mm.wait_ready(act, SETUP, "k", c)
                act.activation(kT_all[:, :, 0, c, :], mm.bank(SETUP, "k", c)[:, 0:B * KEYS].rearrange(
                    "p (b k) -> p b k", b=B), ACT.Copy).then_inc(setup_high, 1)
            for c in range(C):
                tr.wait_ready(act, SETUP, "wv", c)
                tr.read(act.activation(wvT[:, c, :], tr.bank(SETUP, "wv", c), ACT.Copy), SETUP, "wv", c)
            for b in range(B):
                mm.wait_ready(act, SETUP, "v", b)
                mm.read(act.activation(v_all[:, b, :], mm.bank(SETUP, "v", b)[0:KEYS, :], ACT.Copy), SETUP, "v", b)
            for name, w in (("wq", wqT), ("wo", woT)):
                for c in range(C):
                    tr.wait_ready(act, SETUP, name, c)
                    act.activation(w[:, 0, c, :], tr.bank(SETUP, name, c), ACT.Copy, scale=W_SCALE)\
                        .then_inc(setup_high, 1)
            act.wait_ge(ffn_loaded, 16 * (2 * 2 + 3 + 2 * J + 1))
            act.activation(win[:, 0, :, :], win_f[:, :, :, :].rearrange("p c a m -> p c (a m)"), ACT.Copy,
                           scale=W_SCALE).then_inc(win_high, 1)

            def keys(step, batch):
                if isinstance(step.i, int) and step.i == 0:
                    for c in (C - 2, C - 1):
                        mm.wait_read(act, SETUP, "k", c)
                    act.wait_ge(pool_const, 6)
                else:
                    act.wait_ge(lg_ready, HALVES * step.i)
                for j in range(HC):
                    rows = slice(DK * j, DK * (j + 1))
                    act.dma_start(k_blocks[rows, :, :, KEYS * j:KEYS * (j + 1)].rearrange("p a c k -> p (a c) k"),
                                  kT_all[rows, bass.ds(batch, 1), :, :, :].rearrange("p b a c k -> p (b a c) k"))\
                        .then_inc(k_ready, 16)

            def values(step, batch):
                if isinstance(step.i, int) and step.i == 1:
                    for b in (B - 2, B - 1):
                        mm.wait_read(act, SETUP, "v", b)
                else:
                    act.wait_ge(mm_ready, 2 * mm.half(step) - len(mm.order) + C)
                act.dma_start(v_now[:, :], v_all[:, bass.ds(batch, 1), :].rearrange("p a d -> p (a d)"))\
                    .then_inc(v_ready, 16)

            def x_part(step, t):
                tr.wait_ready(act, step, "xT", t)
                act.activation(xT[:, 0, :, P * t:P * (t + 1)], tr.bank(step, "xT", t).rearrange(
                    "p (c r) -> p c r", c=C), ACT.Copy).then_inc(x_high, 1)

            def h_part(step, t):
                tr.wait_ready(act, step, "hT", t)
                act.activation(hT[:, 0, :, P * t:P * (t + 1)], tr.bank(step, "hT", t).rearrange(
                    "p (c r) -> p c r", c=C), ACT.Copy).then_inc(h_high, 1)

            def q_part(step, c):
                mm.wait_ready(act, step, "q", c)
                act.activation(qT[:, step.group(1).parity, 0, c, :], mm.bank(step, "q", c), ACT.Copy)\
                    .then_inc(q_high, 1)

            def exps(step, k):
                g = step.group(0)
                act.wait_ge(lg_free, HALVES * step.i + k + 1)
                p = probs[:, g.parity, k // 2, 8 * KEYS * (k % 2):8 * KEYS * (k % 2 + 1)]
                act.activation(p, p, ACT.Exp, scale=DK ** -0.5 / W_SCALE).then_inc(exp_done, 1)

            def p_copies(step, c):
                for h in range(HC * c, HC * (c + 1)):
                    tr.wait_ready(act, step, "pT", h)
                    tr.read(act.activation(pT[0:KEYS, h % 8, :], tr.bank(step, "pT", h)[0:KEYS, :], ACT.Copy),
                            step, "pT", h)

            def a_part(step, c):
                mm.wait_ready(act, step, "pv", c)
                act.activation(aT[:, 0, c, :], mm.bank(step, "pv", c), ACT.Copy).then_inc(a_high, 1)

            def ffn(step):
                mm.wait_ready(act, step, "s", 0)
                act.activation(s_parts[:, :], mm.bank(step, "s", 0), ACT.Identity, bias=bin16[:, 0:1])\
                    .then_inc(s_high, 1)

            def relus(step):
                for j in range(J):
                    tr.wait_ready(act, step, "pre", j)
                    tr.read(act.activation(inner[:, j % 4, :], tr.bank(step, "pre", j), ACT.Relu,
                                           bias=b1_col[:, j:j + 1], scale=w1_div[:, j:j + 1]), step, "pre", j)
                mm.wait_ready(act, step, "g", 0)
                mm.read(act.activation(gT[:, :], mm.bank(step, "g", 0), ACT.Identity, bias=b2_col[:, 0:1]),
                        step, "g", 0)

            def one_step(step):
                front, soft, back = (part in step.parts for part in (FRONT, SOFT, BACK))
                if soft and step.v % 4 == 0:
                    keys(step, step.t + step.v // 4)
                if back and step.v % 4 == 1 and step.v < GROUPS:
                    values(step, step.t + step.v // 4)
                for c in range(C):
                    if soft:
                        exps(step, c)
                    if back:
                        p_copies(step, c)
                        if c > 0:
                            a_part(step, c - 1)
                if front:
                    x_part(step, 0)
                    x_part(step, 1)
                if back:
                    a_part(step, 3)
                if soft:
                    exps(step, 4)
                if front:
                    x_part(step, 2)
                    x_part(step, 3)
                if soft:
                    exps(step, 5)
                if front:
                    q_part(step, 0)
                    q_part(step, 1)
                if back:
                    h_part(step, 0)
                    h_part(step, 1)
                if soft:
                    exps(step, 6)
                if back:
                    h_part(step, 2)
                    h_part(step, 3)
                if front:
                    q_part(step, 2)
                if soft:
                    exps(step, 7)
                if back:
                    ffn(step)
                if front:
                    q_part(step, 3)
                if back:
                    relus(step)

            run(act, one_step)

        @block.vector
        def _(dve):
            dve.memset(wout[:, :], 0.0).then_inc(ffn_const, 1)
            dve.memset(b2_col[:, :], 0.0).then_inc(zeroed, 1)
            dve.wait_ge(zeroed, 1)
            dve.memset(b2_col[0:DK, :], 1.0).then_inc(ffn_const, 1)
            dve.memset(w2_blocks[:, :, :], 0.0).then_inc(zeroed, 1)
            for c in range(C):
                dve.wait_ge(setup_high, c + 1)
                mm.read(dve.tensor_tensor(
                    kT_all[:, :, 1, c, :], mm.bank(SETUP, "k", c)[:, 0:B * KEYS].rearrange("p (b k) -> p b k", b=B),
                    kT_all[:, :, 0, c, :], ALU.subtract), SETUP, "k", c)
            dve.wait_ge(mask_loaded, 16)
            dve.tensor_scalar(mask_bias[:, :, :, :].rearrange("p g t k -> p g (t k)"), mask_raw, 0, MASKED,
                              ALU.is_equal, ALU.mult).then_inc(mask_ready, 1)
            for n, (name, w) in enumerate((("wq", wqT), ("wo", woT))):
                for c in range(C):
                    dve.wait_ge(setup_high, C * (n + 1) + c + 1)
                    tr.read(dve.scalar_tensor_tensor(w[:, 1, c, :], tr.bank(SETUP, name, c), W_SCALE, w[:, 0, c, :],
                                                     ALU.mult, ALU.subtract), SETUP, name, c)
            dve.wait_ge(ffn_loaded, 16 * (2 * 2 + 3 + 2 * J + 1))
            dve.wait_ge(win_high, 1)
            dve.scalar_tensor_tensor(win[:, 1, :, :], win_f[:, :, :, :].rearrange("p c a m -> p c (a m)"), W_SCALE,
                                     win[:, 0, :, :], ALU.mult, ALU.subtract).then_inc(ffn_const, 1)
            dve.tensor_scalar(bin16[:, :], bin_col[:, :], W_SCALE, None, ALU.mult).then_inc(ffn_const, 1)
            dve.tensor_scalar(w1_div[:, :], w1_col[:, :], 1.0 / W_SCALE, None, ALU.mult).then_inc(ffn_const, 1)
            dve.wait_ge(pool_const, 12)
            dve.wait_ge(zeroed, 2)
            for j in range(J):
                first = MJ * (j // 4)
                dve.tensor_scalar(w2_blocks[:, j, first:first + MJ], units[:, :], w2_col[:, j:j + 1], None, ALU.mult)\
                    .then_inc(ffn_const, 1)

            def x_statistics(step):
                g = step.group(1)
                dve.wait_ge(x_loaded[g.slot], 16 * g.lap + 16)
                for t in range(T):
                    dve.bn_stats(stats[:, 0, t, :], xr[:, g.slot, t, :]).then_inc(x_stats, 1)

            def x_means(step):
                for t in range(T):
                    dve.bn_aggr(mean_var[:, 0, t, :], stats[:, 0, t, :]).then_inc(x_mean, 1)
                dve.wait_ge(x_mean, 4 * step.group(1).n + 4)
                dve.tensor_scalar(var_eps[:, 0, :], mean_var[:, 0, :, 1], EPS, None, ALU.add).then_inc(x_eps, 1)

            def x_normal(step, t):
                g = step.group(1)
                dve.wait_ge(x_rstd, g.n + 1)
                dve.tensor_scalar(xn[:, t, :], xr[:, g.slot, t, :], mean_var[:, 0, t, 0:1], rstd[:, 0, t:t + 1],
                                  ALU.subtract, ALU.mult).then_inc(x_norm, 1)

            def x_low(step, t):
                dve.wait_ge(x_high, 4 * step.group(1).n + t + 1)
                rows = slice(P * t, P * (t + 1))
                tr.read(dve.tensor_tensor(xT[:, 1, :, rows], tr.bank(step, "xT", t).rearrange("p (c r) -> p c r", c=C),
                                          xT[:, 0, :, rows], ALU.subtract), step, "xT", t)

            def q_low(step, c):
                g = step.group(1)
                dve.wait_ge(q_high, 4 * g.n + c + 1)
                mm.read(dve.tensor_tensor(qT[:, g.parity, 1, c, :], mm.bank(step, "q", c), qT[:, g.parity, 0, c, :],
                                          ALU.subtract), step, "q", c)

            def logits_of(k):
                return lg_banks[:, k % 2, :, 0:LW].rearrange("p b (h k) -> p b h k", k=KEYS)

            def probs_of(step, k):
                return probs[:, step.group(0).parity, k // 2, 8 * KEYS * (k % 2):8 * KEYS * (k % 2 + 1)].rearrange(
                    "p (b h k) -> p b h k", b=2, h=HC)

            def maxima(step, k):
                n = HALVES * step.i + k
                dve.wait_ge(lg_ready, n + 1)
                dve.tensor_reduce(row_max[:, k % 2, :, :], logits_of(k), AX.X, ALU.max).then_inc(max_done, 1)
                dve.wait_ge(max_done, n + 1)
                dve.tensor_tensor(probs_of(step, k), logits_of(k),
                                  row_max[:, k % 2, :, :].unsqueeze(3).broadcast_to([P, 2, HC, KEYS]),
                                  ALU.subtract).then_inc(lg_free, 1)

            def sums(step, k):
                n = HALVES * step.i + k
                dve.wait_ge(exp_done, n + 1)
                dve.tensor_reduce(row_sum[:, k % 2, :, :], probs_of(step, k), AX.X, ALU.add).then_inc(sum_done, 1)
                dve.wait_ge(sum_done, n + 1)
                dve.reciprocal(row_inv[:, step.group(0).parity, k, :, :], row_sum[:, k % 2, :, :])\
                    .then_inc(inv_done, 1)

            def a_low(step, c):
                dve.wait_ge(a_high, 4 * step.group(-1).n + c + 1)
                mm.read(dve.tensor_tensor(aT[:, 1, c, :], mm.bank(step, "pv", c), aT[:, 0, c, :], ALU.subtract),
                        step, "pv", c)

            def residual(step, t):
                g = step.group(-1)
                h = xr[:, g.slot, t, :]
                mm.wait_ready(dve, step, "wo", t)
                mm.read(dve.scalar_tensor_tensor(h, mm.bank(step, "wo", t), 1.0 / W_SCALE, h, ALU.mult, ALU.add),
                        step, "wo", t)
                mm.wait_read(dve, step, "wo", t)
                dve.bn_stats(stats[:, 1, t, :], h).then_inc(h_stats, 1)

            def h_means(step):
                for t in range(T):
                    dve.bn_aggr(mean_var[:, 1, t, :], stats[:, 1, t, :]).then_inc(h_mean, 1)
                dve.wait_ge(h_mean, 4 * step.group(-1).n + 4)
                dve.tensor_scalar(var_eps[:, 1, :], mean_var[:, 1, :, 1], EPS, None, ALU.add).then_inc(h_eps, 1)

            def h_normal(step, t):
                g = step.group(-1)
                dve.wait_ge(h_rstd, g.n + 1)
                dve.tensor_scalar(hn[:, t, :], xr[:, g.slot, t, :], mean_var[:, 1, t, 0:1], rstd[:, 1, t:t + 1],
                                  ALU.subtract, ALU.mult).then_inc(h_norm, 1)

            def h_low(step, t):
                dve.wait_ge(h_high, 4 * step.group(-1).n + t + 1)
                rows = slice(P * t, P * (t + 1))
                tr.read(dve.tensor_tensor(hT[:, 1, :, rows], tr.bank(step, "hT", t).rearrange("p (c r) -> p c r", c=C),
                                          hT[:, 0, :, rows], ALU.subtract), step, "hT", t)

            def s_low(step):
                dve.wait_ge(s_high, step.group(-1).n + 1)
                low = s_parts[M:2 * M, :]
                mm.read(dve.scalar_tensor_tensor(low, mm.bank(step, "s", 0)[M:2 * M, :], bin16[M:2 * M, 0:1], low,
                                                 ALU.add, ALU.subtract), step, "s", 0)

            def outputs(step):
                g = step.group(-1)
                for t in range(T):
                    h = xr[:, g.slot, t, :]
                    mm.wait_ready(dve, step, "out", t)
                    mm.read(dve.tensor_tensor(h, mm.bank(step, "out", t), h, ALU.add), step, "out", t)

            def one_step(step):
                front, soft, back = (part in step.parts for part in (FRONT, SOFT, BACK))
                if soft:
                    maxima(step, 0)
                if front:
                    x_statistics(step)
                for c in range(1, C):
                    if front and c == 1:
                        dve.wait_ge(x_stats, 4 * step.group(1).n + 4)
                    if soft:
                        maxima(step, c)
                    if front and c == 1:
                        x_means(step)
                    if soft:
                        sums(step, c - 1)
                    if back:
                        a_low(step, c - 1)
                    if front and c == 2:
                        x_normal(step, 0)
                        x_normal(step, 1)
                if front:
                    x_normal(step, 2)
                    x_normal(step, 3)
                    x_low(step, 0)
                    x_low(step, 1)
                if back:
                    a_low(step, 3)
                if soft:
                    maxima(step, 4)
                    sums(step, 3)
                if back:
                    residual(step, 0)
                    residual(step, 1)
                if front:
                    x_low(step, 2)
                if back:
                    residual(step, 2)
                    residual(step, 3)
                    dve.wait_ge(h_stats, 4 * step.group(-1).n + 4)
                if front:
                    x_low(step, 3)
                if back:
                    h_means(step)
                if soft:
                    maxima(step, 5)
                    sums(step, 4)
                if front:
                    q_low(step, 0)
                    q_low(step, 1)
                if back:
                    for t in range(T):
                        h_normal(step, t)
                    h_low(step, 0)
                    h_low(step, 1)
                if soft:
                    maxima(step, 6)
                    sums(step, 5)
                if back:
                    h_low(step, 2)
                    h_low(step, 3)
                if front:
                    q_low(step, 2)
                if soft:
                    maxima(step, 7)
                    sums(step, 6)
                if back:
                    s_low(step)
                if front:
                    q_low(step, 3)
                if soft:
                    sums(step, 7)
                if back:
                    outputs(step)

            run(dve, one_step)

        @block.tensor
        def _(pe):
            pe.wait_ge(pool_const, 4)

            pe.wait_ge(ctx_loaded, 16)
            for c in range(C):
                tr.wait_free(pe, SETUP, "ctxT", c)
                bank = tr.bank(SETUP, "ctxT", c)
                for b in range(B):
                    last = pe.transpose(bank[:, KEYS * b:KEYS * (b + 1)], ctx_raw[:, b, P * c:P * (c + 1)],
                                        ident[0:KEYS, 0:KEYS])
                last.then_inc(tr_ready, 1)

            def weight(n, name):
                pe.wait_ge(w_loaded[n], 16)
                for c in range(C):
                    tr.wait_free(pe, SETUP, name, c)
                    bank = tr.bank(SETUP, name, c)
                    for o in range(C):
                        last = pe.transpose(bank[:, P * o:P * (o + 1)], w_raw[:, n, o, P * c:P * (c + 1)], ident[:, :])
                    last.then_inc(tr_ready, 1)

            weight(0, "wk")
            for c in range(C):
                tr.wait_read(pe, SETUP, "wk", c)
            for o in range(C):
                mm.wait_free(pe, SETUP, "k", o)
                for c in range(C):
                    last = pe.matmul(mm.bank(SETUP, "k", o)[:, 0:B * KEYS], wkT[:, c, P * o:P * (o + 1)],
                                     ctxT[:, c, :], start=(c == 0), stop=(c == C - 1))
                last.then_inc(mm_ready, 1)
            weight(1, "wv")
            for c in range(C):
                tr.wait_read(pe, SETUP, "wv", c)
            for b in range(B):
                mm.wait_free(pe, SETUP, "v", b)
                for c in range(C):
                    last = pe.matmul(mm.bank(SETUP, "v", b)[0:KEYS, :], ctxT[:, c, KEYS * b:KEYS * (b + 1)],
                                     wvT[:, c, :], start=(c == 0), stop=(c == C - 1))
                last.then_inc(mm_ready, 1)
            weight(2, "wq")
            weight(3, "wo")

            def three_passes(bank, stationary, moving, chunks):
                passes = [(c, a, b) for c in range(chunks) for a, b in ((0, 0), (0, 1), (1, 0))]
                for n, (c, a, b) in enumerate(passes):
                    last = pe.matmul(bank, stationary(a, c), moving(b, c), start=(n == 0),
                                     stop=(n == len(passes) - 1))
                return last

            def x_transpose(step, t):
                g = step.group(1)
                tr.wait_free(pe, step, "xT", t)
                pe.wait_ge(x_norm, 4 * g.n + t + 1)
                for c in range(C):
                    last = pe.transpose(tr.bank(step, "xT", t)[:, P * c:P * (c + 1)], xn[:, t, P * c:P * (c + 1)],
                                        ident[:, :])
                last.then_inc(tr_ready, 1)

            def q(step, o):
                if o == 0:
                    for t in (T - 2, T - 1):
                        tr.wait_read(pe, step, "xT", t)
                    if not isinstance(step.i, int) or step.i >= 0:
                        pass
                    else:
                        for c in (C - 2, C - 1):
                            tr.wait_read(pe, SETUP, "wq", c)
                mm.wait_free(pe, step, "q", o)
                three_passes(mm.bank(step, "q", o), lambda a, c: wqT[:, a, c, P * o:P * (o + 1)],
                             lambda b, c: xT[:, b, c, :], C).then_inc(mm_ready, 1)

            def logits(step, k):
                n = HALVES * step.i + k
                g = step.group(0)
                t, u = k // 2, k % 2
                if k == 0:
                    if isinstance(step.i, int) and step.i == 0:
                        pe.wait_ge(mask_ready, 1)
                    before = Step(step.t, step.v - 1, (FRONT,) if step.v == 0 and isinstance(step.i, int) else
                                  (FRONT, SOFT) if isinstance(step.i, int) and step.i == 1 else (FRONT, SOFT, BACK))
                    if not isinstance(step.i, int) and step.v == 1:
                        for b in range(2):
                            pe.wait_ge(mm_free[b], mm.half(step))
                    else:
                        for c in (2, 3):
                            mm.wait_read(pe, before, "q", c)
                    if step.v % 4 == 0:
                        pe.wait_ge(k_ready, 16 * HC * (step.t + step.v // 4 + 1))
                if not (isinstance(n, int) and n < 2):
                    pe.wait_ge(lg_free, n - 1)
                rows = slice(P * t, P * (t + 1))
                for b in range(2):
                    c = 2 * u + b
                    bank = lg_banks[:, k % 2, b, 0:LW]
                    for m, (qp, kp) in enumerate(((0, 0), (0, 1), (1, 0))):
                        pe.matmul(bank, qT[:, g.parity, qp, c, rows], k_blocks[:, kp, c, :], start=(m == 0), stop=False)
                    last = pe.matmul(bank.rearrange("p (h k) -> p h k", k=KEYS), ident_bf[:, :],
                                     mask_bias[:, g.slot, t, :].unsqueeze(1).broadcast_to([P, HC, KEYS]),
                                     start=False, stop=True)
                last.then_inc(lg_ready, 1)

            def p_transposes(step, c):
                g = step.group(-1)
                if c == 0:
                    pe.wait_ge(probs_ready, HALVES * g.n + HALVES)
                for h in range(HC * c, HC * (c + 1)):
                    tr.wait_free(pe, step, "pT", h)
                    for t in range(T):
                        last = pe.transpose(tr.bank(step, "pT", h)[0:KEYS, P * t:P * (t + 1)],
                                            probs[:, g.parity, t, KEYS * h:KEYS * (h + 1)], ident[:, :])
                    last.then_inc(tr_ready, 1)

            def pv(step, c):
                if c == 0 and step.v % 4 == 1:
                    pe.wait_ge(v_ready, 16 * (step.t + step.v // 4 + 1))
                for h in (2, 3):
                    tr.wait_read(pe, step, "pT", HC * c + h)
                mm.wait_free(pe, step, "pv", c)
                for h in range(HC):
                    last = pe.matmul(mm.bank(step, "pv", c)[DK * h:DK * (h + 1), :],
                                     v_now[:, DK * (HC * c + h):DK * (HC * c + h + 1)], pT[0:KEYS, (HC * c + h) % 8, :],
                                     start=True, stop=True)
                last.then_inc(mm_ready, 1)

            def wo(step, t):
                if t == 0:
                    for c in (C - 2, C - 1):
                        mm.wait_read(pe, step, "pv", c)
                    if isinstance(step.i, int) and step.i == 1:
                        pass
                mm.wait_free(pe, step, "wo", t)
                three_passes(mm.bank(step, "wo", t), lambda a, c: aT[:, a, c, P * t:P * (t + 1)],
                             lambda b, c: woT[:, b, c, :], C).then_inc(mm_ready, 1)

            def h_transpose(step, t):
                tr.wait_free(pe, step, "hT", t)
                pe.wait_ge(h_norm, 4 * step.group(-1).n + t + 1)
                for c in range(C):
                    last = pe.transpose(tr.bank(step, "hT", t)[:, P * c:P * (c + 1)], hn[:, t, P * c:P * (c + 1)],
                                        ident[:, :])
                last.then_inc(tr_ready, 1)

            def ffn_in(step):
                for t in (T - 2, T - 1):
                    tr.wait_read(pe, step, "hT", t)
                mm.wait_free(pe, step, "s", 0)
                three_passes(mm.bank(step, "s", 0), lambda a, c: win[:, a, c, :], lambda b, c: hT[:, b, c, :], C)\
                    .then_inc(mm_ready, 1)

            def ffn_pre(step, j):
                if j == 0:
                    mm.wait_read(pe, step, "s", 0)
                tr.wait_free(pe, step, "pre", j)
                pe.matmul(tr.bank(step, "pre", j), spread[:, j, :], s_parts[:, :], start=True, stop=True)\
                    .then_inc(tr_ready, 1)

            def ffn_g(step, j):
                if j == 0:
                    mm.wait_free(pe, step, "g", 0)
                tr.wait_read(pe, step, "pre", j)
                group = DK * (j % 4)
                last = pe.matmul(mm.bank(step, "g", 0)[group:group + DK, :], w2_blocks[:, j, :], inner[:, j % 4, :],
                                 start=(j < 4), stop=(j >= 4))
                if j == J - 1:
                    last.then_inc(mm_ready, 1)

            def ffn_out(step, t):
                if t == 0:
                    mm.wait_read(pe, step, "g", 0)
                mm.wait_free(pe, step, "out", t)
                pe.matmul(mm.bank(step, "out", t), gT[:, P * t:P * (t + 1)], wout[:, :], start=True, stop=True)\
                    .then_inc(mm_ready, 1)

            def one_step(step):
                front, soft, back = (part in step.parts for part in (FRONT, SOFT, BACK))
                for c in range(C):
                    if soft:
                        logits(step, c)
                    if back:
                        p_transposes(step, c)
                        if c > 0:
                            pv(step, c - 1)
                if front:
                    x_transpose(step, 0)
                    x_transpose(step, 1)
                if back:
                    pv(step, 3)
                if soft:
                    logits(step, 4)
                if back:
                    wo(step, 0)
                    wo(step, 1)
                if front:
                    x_transpose(step, 2)
                    x_transpose(step, 3)
                if back:
                    wo(step, 2)
                    wo(step, 3)
                if soft:
                    logits(step, 5)
                if front:
                    q(step, 0)
                    q(step, 1)
                if back:
                    h_transpose(step, 0)
                    h_transpose(step, 1)
                if soft:
                    logits(step, 6)
                if back:
                    h_transpose(step, 2)
                    h_transpose(step, 3)
                if front:
                    q(step, 2)
                if soft:
                    logits(step, 7)
                if back:
                    ffn_in(step)
                if front:
                    q(step, 3)
                if back:
                    for j in range(J + 2):
                        if j < J:
                            ffn_pre(step, j)
                        if j >= 2:
                            ffn_g(step, j - 2)
                    for t in range(T):
                        ffn_out(step, t)
                if isinstance(step.i, int) and step.i == -1:
                    pe.wait_ge(ffn_const, 5 + J)
                    pe.wait_ge(pool_const, 12)
                    for c in (C - 2, C - 1):
                        tr.wait_read(pe, SETUP, "wo", c)

            run(pe, one_step)


_INS = ['x', 'ctx_1024', 'mask_1x1xSxS2_ik0', 'L0_xattn_Wq', 'L0_xattn_Wk', 'L0_xattn_Wv', 'L0_xattn_Wo',
        'L0_ffn_Win', 'L0_ffn_bin_', 'L0_ffn_W1', 'L0_ffn_b1', 'L0_ffn_W2', 'L0_ffn_b2', 'L0_ffn_Wout', 'L0_ffn_bout']


def kernel(**inputs):
    import numpy as _np
    import concourse.bacc as _bacc
    from concourse import mybir as _mybir
    from concourse.bass_utils import run_bass_kernel_spmd as _run

    nc = _bacc.Bacc("TRN2", target_bir_lowering=False, num_devices=1)
    arrays, args = {}, []
    for name in _INS:
        a = _np.ascontiguousarray(inputs[name])
        arrays[f"in_{name}"] = a
        args.append(nc.dram_tensor(f"in_{name}", a.shape, _mybir.dt.from_np(a.dtype), kind="ExternalInput").ap())
    args.append(nc.dram_tensor("out_x", (B, S, D), _mybir.dt.float32, kind="ExternalOutput").ap())
    build(nc, *args)
    r = _run(nc, [arrays], core_ids=[0])
    return r.results[0]["out_x"]
```

```python
from contextlib import ExitStack

import concourse.bass as bass
from concourse import mybir

F32 = mybir.dt.float32
F16 = mybir.dt.float16
BF16 = mybir.dt.bfloat16
I32 = mybir.dt.int32
ALU = mybir.AluOpType
ACT = mybir.ActivationFunctionType
AX = mybir.AxisListType

P = 128
D = 512
C = D // P
B = 4
S = 2048
T = 4
ROWS = T * P
GROUPS = B * S // ROWS
PER_BATCH = GROUPS // B
KEYS = 77
HEADS = 16
DK = D // HEADS
HC = P // DK
LW = HC * KEYS
HALVES = 2 * T
M = 64
INNER = 16
J = M * INNER // P
MJ = M // J
W_SCALE = 16.0
MASKED = -(2.0 ** 100)
EPS = 1e-5

SETUP, FRONT, SOFT, BACK, FFN = "setup", "front", "soft", "back", "ffn"
ALL = (FRONT, SOFT, BACK, FFN)
FIRST_FULL = 2
LOOPED = 4 * (GROUPS // 4 - 1)

TR_SETUP = [("ctxT", c) for c in range(C)] + [(w, c) for w in ("wk", "wv", "wq", "wo") for c in range(C)]
TR_ORDER = (
    [use for c in range(C)
     for use in [(BACK, "pT", h) for h in range(HC * c, HC * (c + 1))] + [(FFN, "pre", 2 * c), (FFN, "pre", 2 * c + 1)]]
    + [(FRONT, "xT", t) for t in range(T)]
    + [(BACK, "hT", t) for t in range(T)]
)
MM_SETUP = [("k", c) for c in range(C)] + [("v", b) for b in range(B)]
MM_ORDER = (
    [(FFN, "s", 0)]
    + [(BACK, "pv", c) for c in range(C)]
    + [(FFN, "g", 0), (BACK, "wo", 0), (BACK, "wo", 1), (FFN, "out", 0), (BACK, "wo", 2), (FFN, "out", 1),
       (BACK, "wo", 3), (FFN, "out", 2), (FFN, "out", 3)]
    + [(FRONT, "q", c) for c in range(C)]
)


def parts_of(i):
    return tuple(part for part, ahead in zip(ALL, (1, 0, -1, -2)) if 0 <= i + ahead < GROUPS)


class Step:

    def __init__(self, t, v):
        self.t, self.v = t, v
        self.i = 4 * t + v
        self.parts = parts_of(self.i) if isinstance(self.i, int) else ALL

    def first(self, i):
        return isinstance(self.i, int) and self.i == i

    def group(self, ahead):
        return Group(self.t, self.v + ahead)


class Group:

    def __init__(self, t, v):
        self.n, self.slot, self.lap, self.parity = 4 * t + v, v % 4, t + v // 4, v % 2


class Ring:

    def __init__(self, setup, order, tensor, ready, free):
        self.setup, self.order, self.tensor, self.ready, self.free = setup, order, tensor, ready, free

    def half(self, step):
        def uses(i):
            return sum(part in parts_of(i) for part, _, _ in self.order)

        if step is SETUP:
            return 0
        if isinstance(step.i, int):
            return (len(self.setup) + sum(uses(i) for i in range(-1, step.i))) // 2
        before = (len(self.setup) + sum(uses(i) for i in range(-1, FIRST_FULL))) // 2
        return before + (step.i - FIRST_FULL) * (len(self.order) // 2)

    def place(self, step, name, k):
        if step is SETUP:
            return self.setup.index((name, k))
        return [(n, m) for part, n, m in self.order if part in step.parts].index((name, k))

    def bank(self, step, name, k):
        return self.tensor[:, self.place(step, name, k) % 2, :]

    def wait_free(self, eng, step, name, k):
        place = self.place(step, name, k)
        value = self.half(step) + place // 2
        if not (isinstance(value, int) and value < 1):
            eng.wait_ge(self.free[place % 2], value)

    def wait_ready(self, eng, step, name, k):
        eng.wait_ge(self.ready, 2 * self.half(step) + self.place(step, name, k) + 1)

    def wait_read(self, eng, step, name, k):
        place = self.place(step, name, k)
        eng.wait_ge(self.free[place % 2], self.half(step) + place // 2 + 1)

    def wait_all_read(self, eng, step, but=0):
        for b in range(2):
            eng.wait_ge(self.free[b], self.half(step) - but)

    def read(self, instruction, step, name, k):
        instruction.then_inc(self.free[self.place(step, name, k) % 2], 1)


def build(nc, x, ctx_in, mask, Wq, Wk, Wv, Wo, Win, bin_, W1, b1, W2, b2, Wout, bout, out):
    stack = ExitStack()
    with stack:
        def sb(name, shape, dt):
            return stack.enter_context(nc.sbuf_tensor(name, shape, dt))

        def sem(name):
            return stack.enter_context(nc.semaphore(name))

        tr_banks = stack.enter_context(nc.psum_tensor("tr_banks", [P, 2, D], F32))
        mm_banks = stack.enter_context(nc.psum_tensor("mm_banks", [P, 2, D], F32))
        lg_banks = stack.enter_context(nc.psum_tensor("lg_banks", [P, 2, 2, 512], F32))

        ident = sb("ident", [P, P], F32)
        ident_bf = sb("ident_bf", [P, P], BF16)
        wqT = sb("wqT", [P, 2, C, D], F16)
        woT = sb("woT", [P, 2, C, D], F16)
        win_f = sb("win_f", [P, C, 2, M], F32)
        win = sb("win", [P, 2, C, 2 * M], F16)
        kT_all = sb("kT_all", [P, B, 2, C, KEYS], F16)
        k_blocks = sb("k_blocks", [P, 2, C, LW], F16)
        v_all = sb("v_all", [KEYS, B, D], F32)
        v_now = sb("v_now", [KEYS, D], F32)
        mask_bias = sb("mask_bias", [P, PER_BATCH, T, KEYS], BF16)
        spread = sb("spread", [P, J, P], F16)
        w1_col = sb("w1_col", [P, J], F32)
        w1_div = sb("w1_div", [P, J], F32)
        b1_col = sb("b1_col", [P, J], F32)
        w2_col = sb("w2_col", [P, J], F32)
        units = sb("units", [P, MJ], F32)
        w2_blocks = sb("w2_blocks", [P, J, DK], F32)
        bin_col = sb("bin_col", [P, 1], F32)
        bin16 = sb("bin16", [P, 1], F32)
        b2_col = sb("b2_col", [P, 1], F32)
        wout = sb("wout", [P, D], F32)
        neg_half = sb("neg_half", [P, T], F32)

        xr = sb("xr", [P, 4, T, D], F32)
        normed = sb("normed", [P, T, D], F32)
        xT = sb("xT", [P, 2, C, ROWS], F16)
        hT = sb("hT", [P, 2, C, ROWS], F16)
        qT = sb("qT", [P, 2, 2, C, ROWS], F16)
        probs = sb("probs", [P, 2, T, HEADS * KEYS], F32)
        pT = sb("pT", [P, 8, ROWS], F32)
        aT = sb("aT", [P, 2, C, ROWS], F16)
        s_parts = sb("s_parts", [P, ROWS], F16)
        inner = sb("inner", [P, J, ROWS], F32)
        gT = sb("gT", [P, ROWS], F32)
        stats = sb("stats", [P, 2, T, 6], F32)
        mean_var = sb("mean_var", [P, 2, T, 2], F32)
        var_eps = sb("var_eps", [P, 2, T], F32)
        rstd = sb("rstd", [P, 2, T], F32)
        row_max = sb("row_max", [P, 2, 2, HC], F32)
        row_sum = sb("row_sum", [P, 2, 2, HC], F32)
        row_inv = sb("row_inv", [P, 2, HALVES, 2, HC], F32)

        w_raw = probs[:, :, :, :].rearrange("p a t n -> p (a t n)")[:, 0:4 * C * D].rearrange(
            "p (w c n) -> p w c n", w=4, c=C)
        wkT = pT[:, 0:4, :]
        wvT = pT[:, 4:8, :]
        ctxT = xr[:, 2, :, 0:B * KEYS]
        ctx_raw = xr[0:KEYS, 3, :, :]
        mask_raw = normed[:, :, 0:T * KEYS].bitcast(I32)

        ctx_loaded = sem("ctx_loaded")
        w_loaded = [sem(f"w_loaded_{w}") for w in ("k", "v", "q", "o")]
        mask_loaded = sem("mask_loaded")
        ffn_loaded = sem("ffn_loaded")
        x_loaded = [sem(f"x_loaded_{s}") for s in range(4)]
        out_stored = [sem(f"out_stored_{s}") for s in range(4)]
        pool_const = sem("pool_const")
        ffn_const = sem("ffn_const")
        mask_ready = sem("mask_ready")
        zeroed = sem("zeroed")
        tr_ready = sem("tr_ready")
        mm_ready = sem("mm_ready")
        lg_ready = sem("lg_ready")
        tr_free = [sem("tr_free_0"), sem("tr_free_1")]
        mm_free = [sem("mm_free_0"), sem("mm_free_1")]
        lg_free = sem("lg_free")
        setup_high = sem("setup_high")
        win_high = sem("win_high")
        x_stats = sem("x_stats")
        x_mean = sem("x_mean")
        x_eps = sem("x_eps")
        x_rstd = sem("x_rstd")
        x_norm = sem("x_norm")
        x_high = sem("x_high")
        q_high = sem("q_high")
        max_done = sem("max_done")
        exp_done = sem("exp_done")
        sum_done = sem("sum_done")
        inv_done = sem("inv_done")
        probs_ready = sem("probs_ready")
        k_ready = sem("k_ready")
        v_ready = sem("v_ready")
        a_high = sem("a_high")
        h_stats = sem("h_stats")
        h_mean = sem("h_mean")
        h_eps = sem("h_eps")
        h_rstd = sem("h_rstd")
        h_norm = sem("h_norm")
        h_high = sem("h_high")
        s_high = sem("s_high")

        tr = Ring(TR_SETUP, TR_ORDER, tr_banks, tr_ready, tr_free)
        mm = Ring(MM_SETUP, MM_ORDER, mm_banks, mm_ready, mm_free)

        x_rows = x.rearrange("b (g p t) d -> (b g) p t d", p=P, t=T)
        out_rows = out.rearrange("b (g p t) d -> (b g) p t d", p=P, t=T)

        def run(eng, one_step):
            for i in range(-1, FIRST_FULL):
                one_step(Step(0, i))
            with eng.Fori(0, LOOPED // 4, 1) as t:
                for v in range(FIRST_FULL, FIRST_FULL + 4):
                    one_step(Step(t, v))
            for i in range(FIRST_FULL + LOOPED, GROUPS + 2):
                one_step(Step(0, i))

        block = stack.enter_context(nc.Block())

        @block.sync
        def _(sp):
            sp.dma_start(ctx_raw, ctx_in.rearrange("b k d -> k b d")).then_inc(ctx_loaded, 16)
            for n, w in enumerate((Wk, Wv, Wq, Wo)):
                sp.dma_start(w_raw[:, n, :, :], w.rearrange("(c p) n -> p c n", p=P)).then_inc(w_loaded[n], 16)
            for n in range(2):
                sp.dma_start(xr[:, n, :, :], x_rows[n]).then_inc(x_loaded[n], 16)
            mm.wait_ready(sp, SETUP, "v", B - 1)
            for n in range(2, 4):
                sp.dma_start(xr[:, n, :, :], x_rows[n]).then_inc(x_loaded[n], 16)

            def store(step):
                g = step.group(-2)
                mm.wait_read(sp, step, "out", T - 2)
                mm.wait_read(sp, step, "out", T - 1)
                sp.dma_start(out_rows[g.n], xr[:, g.slot, :, :]).then_inc(out_stored[g.slot], 16)

            def load(step):
                g = step.group(2)
                sp.wait_ge(out_stored[g.slot], 16 * g.lap)
                sp.dma_start(xr[:, g.slot, :, :], x_rows[g.n]).then_inc(x_loaded[g.slot], 16)

            with sp.Fori(0, LOOPED // 4, 1) as t:
                for v in range(FIRST_FULL, FIRST_FULL + 4):
                    store(Step(t, v))
                    load(Step(t, v))
            for i in range(FIRST_FULL + LOOPED, GROUPS + 2):
                store(Step(0, i))
            for s in range(4):
                sp.wait_ge(out_stored[s], 16 * (GROUPS // 4))

        @block.gpsimd
        def _(pool):
            pool.memset(ident[:, :], 0.0).then_inc(pool_const, 1)
            pool.memset(ident_bf[:, :], 0.0).then_inc(pool_const, 1)
            pool.wait_ge(pool_const, 2)
            for m in (ident, ident_bf):
                pool.affine_select(out=m[:, :], in_=m[:, :], compare_op=ALU.not_equal, fill=1.0, base=0,
                                   pattern=[[-1, P]], channel_multiplier=1).then_inc(pool_const, 1)
            pool.memset(neg_half[:, :], -0.5).then_inc(pool_const, 1)
            pool.memset(k_blocks[:, :, :, :], 0.0).then_inc(pool_const, 1)
            pool.memset(spread[:, :, :], 0.0).then_inc(pool_const, 1)
            pool.memset(units[:, :], 1.0).then_inc(pool_const, 1)
            for n, first in enumerate((0, -M)):
                pool.wait_ge(pool_const, 8 + n)
                v = spread[:, :, :].rearrange("p j (i n) -> p j i n", n=INNER)
                pool.affine_select(out=v, in_=v, compare_op=ALU.not_equal, fill=1.0, base=first,
                                   pattern=[[-MJ, J], [-1, MJ], [0, INNER]], channel_multiplier=1)\
                    .then_inc(pool_const, 1)
            pool.wait_ge(pool_const, 10)
            pool.affine_select(out=units[:, :], in_=units[:, :], compare_op=ALU.is_ge, fill=0.0, base=0,
                               pattern=[[-INNER, MJ]], channel_multiplier=1).then_inc(pool_const, 1)
            pool.wait_ge(pool_const, 11)
            pool.affine_select(out=units[:, :], in_=units[:, :], compare_op=ALU.is_ge, fill=0.0, base=INNER - 1,
                               pattern=[[INNER, MJ]], channel_multiplier=-1).then_inc(pool_const, 1)

            def front(step):
                n = step.i + 1
                pool.wait_ge(x_eps, n + 1)
                pool.tensor_tensor(rstd[:, 0, :], var_eps[:, 0, :], neg_half[:, :], ALU.pow).then_inc(x_rstd, 1)

            def back_rstd(step):
                n = step.i - 1
                pool.wait_ge(h_eps, n + 1)
                pool.tensor_tensor(rstd[:, 1, :], var_eps[:, 1, :], neg_half[:, :], ALU.pow).then_inc(h_rstd, 1)

            def divide(step, k):
                n = HALVES * step.i + k
                g = step.group(0)
                t, u = k // 2, k % 2
                pool.wait_ge(inv_done, n + 1)
                p = probs[:, g.parity, t, 8 * KEYS * u:8 * KEYS * (u + 1)].rearrange("p (b h k) -> p b h k", b=2, h=HC)
                inv = row_inv[:, g.parity, k, :, :].unsqueeze(3).broadcast_to([P, 2, HC, KEYS])
                pool.tensor_tensor(p, p, inv, ALU.mult).then_inc(probs_ready, 1)

            def one_step(step):
                if FRONT in step.parts:
                    front(step)
                if SOFT in step.parts:
                    for k in range(5):
                        divide(step, k)
                if BACK in step.parts:
                    back_rstd(step)
                if SOFT in step.parts:
                    for k in range(5, HALVES):
                        divide(step, k)

            run(pool, one_step)

        @block.scalar
        def _(act):
            act.dma_start(mask_raw, mask[0, 0].rearrange("(g p t) k -> p g (t k)", p=P, t=T)).then_inc(mask_loaded, 16)
            for twice in range(2):
                act.dma_start(win_f[:, :, twice, :], Win.rearrange("(c p) m -> p c m", p=P)).then_inc(ffn_loaded, 16)
                act.dma_start(bin_col[M * twice:M * (twice + 1), :], bin_.rearrange("(m a) -> m a", a=1))\
                    .then_inc(ffn_loaded, 16)
            for col, w in ((w1_col, W1), (b1_col, b1), (w2_col, W2)):
                act.dma_start(col[:, :], w.rearrange("(j i) n -> (i n) j", i=MJ), allow_slow_non_contiguous=True)\
                    .then_inc(ffn_loaded, 16)
            act.wait_ge(ffn_const, 2)
            for j in range(J):
                first = DK * (j % 4) + MJ * (j // 4)
                act.dma_start(wout[first:first + MJ, :], Wout[MJ * j:MJ * (j + 1), :]).then_inc(ffn_loaded, 16)
                act.dma_start(b2_col[first:first + MJ, :], b2[MJ * j:MJ * (j + 1)].rearrange("(m a) -> m a", a=1))\
                    .then_inc(ffn_loaded, 16)
            act.dma_start(wout[2 * MJ:2 * MJ + 1, :], bout.rearrange("(a d) -> a d", a=1)).then_inc(ffn_loaded, 16)

            for c in range(C):
                tr.wait_ready(act, SETUP, "ctxT", c)
                tr.read(act.activation(ctxT[:, c, :], tr.bank(SETUP, "ctxT", c)[:, 0:B * KEYS], ACT.Copy),
                        SETUP, "ctxT", c)
            for c in range(C):
                tr.wait_ready(act, SETUP, "wk", c)
                tr.read(act.activation(wkT[:, c, :], tr.bank(SETUP, "wk", c), ACT.Copy), SETUP, "wk", c)
            for c in range(C):
                mm.wait_ready(act, SETUP, "k", c)
                act.activation(kT_all[:, :, 0, c, :], mm.bank(SETUP, "k", c)[:, 0:B * KEYS].rearrange(
                    "p (b k) -> p b k", b=B), ACT.Copy).then_inc(setup_high, 1)
            for c in range(C):
                tr.wait_ready(act, SETUP, "wv", c)
                tr.read(act.activation(wvT[:, c, :], tr.bank(SETUP, "wv", c), ACT.Copy), SETUP, "wv", c)
            for b in range(B):
                mm.wait_ready(act, SETUP, "v", b)
                mm.read(act.activation(v_all[:, b, :], mm.bank(SETUP, "v", b)[0:KEYS, :], ACT.Copy), SETUP, "v", b)
            for name, w in (("wq", wqT), ("wo", woT)):
                for c in range(C):
                    tr.wait_ready(act, SETUP, name, c)
                    act.activation(w[:, 0, c, :], tr.bank(SETUP, name, c), ACT.Copy, scale=W_SCALE)\
                        .then_inc(setup_high, 1)
            act.wait_ge(ffn_loaded, 16 * (2 * 2 + 3 + 2 * J + 1))
            act.activation(win[:, 0, :, :], win_f[:, :, :, :].rearrange("p c a m -> p c (a m)"), ACT.Copy,
                           scale=W_SCALE).then_inc(win_high, 1)

            def keys(step, batch):
                if step.first(0):
                    for c in (C - 2, C - 1):
                        mm.wait_read(act, SETUP, "k", c)
                    act.wait_ge(pool_const, 6)
                else:
                    act.wait_ge(lg_ready, HALVES * step.i)
                for j in range(HC):
                    rows = slice(DK * j, DK * (j + 1))
                    act.dma_start(k_blocks[rows, :, :, KEYS * j:KEYS * (j + 1)].rearrange("p a c k -> p (a c) k"),
                                  kT_all[rows, bass.ds(batch, 1), :, :, :].rearrange("p b a c k -> p (b a c) k"))\
                        .then_inc(k_ready, 16)

            def values(step, batch):
                if step.first(1):
                    for b in (B - 2, B - 1):
                        mm.wait_read(act, SETUP, "v", b)
                else:
                    mm.wait_ready(act, Step(step.t, step.v - 1), "pv", C - 1)
                act.dma_start(v_now[:, :], v_all[:, bass.ds(batch, 1), :].rearrange("p a d -> p (a d)"))\
                    .then_inc(v_ready, 16)

            def x_part(step, t):
                tr.wait_ready(act, step, "xT", t)
                act.activation(xT[:, 0, :, P * t:P * (t + 1)], tr.bank(step, "xT", t).rearrange(
                    "p (c r) -> p c r", c=C), ACT.Copy).then_inc(x_high, 1)

            def h_part(step, t):
                tr.wait_ready(act, step, "hT", t)
                act.activation(hT[:, 0, :, P * t:P * (t + 1)], tr.bank(step, "hT", t).rearrange(
                    "p (c r) -> p c r", c=C), ACT.Copy).then_inc(h_high, 1)

            def q_part(step, c):
                mm.wait_ready(act, step, "q", c)
                act.activation(qT[:, step.group(1).parity, 0, c, :], mm.bank(step, "q", c), ACT.Copy)\
                    .then_inc(q_high, 1)

            def exps(step, k):
                g = step.group(0)
                act.wait_ge(lg_free, HALVES * step.i + k + 1)
                p = probs[:, g.parity, k // 2, 8 * KEYS * (k % 2):8 * KEYS * (k % 2 + 1)]
                act.activation(p, p, ACT.Exp, scale=DK ** -0.5 / W_SCALE).then_inc(exp_done, 1)

            def p_copies(step, c):
                for h in range(HC * c, HC * (c + 1)):
                    tr.wait_ready(act, step, "pT", h)
                    tr.read(act.activation(pT[0:KEYS, h % 8, :], tr.bank(step, "pT", h)[0:KEYS, :], ACT.Copy),
                            step, "pT", h)

            def a_part(step, c):
                mm.wait_ready(act, step, "pv", c)
                act.activation(aT[:, 0, c, :], mm.bank(step, "pv", c), ACT.Copy).then_inc(a_high, 1)

            def s_part(step):
                mm.wait_ready(act, step, "s", 0)
                act.activation(s_parts[:, :], mm.bank(step, "s", 0), ACT.Identity, bias=bin16[:, 0:1])\
                    .then_inc(s_high, 1)

            def relus(step, c):
                for j in (2 * c, 2 * c + 1):
                    tr.wait_ready(act, step, "pre", j)
                    tr.read(act.activation(inner[:, j, :], tr.bank(step, "pre", j), ACT.Relu,
                                           bias=b1_col[:, j:j + 1], scale=w1_div[:, j:j + 1]), step, "pre", j)

            def g_copy(step):
                mm.wait_ready(act, step, "g", 0)
                mm.read(act.activation(gT[:, :], mm.bank(step, "g", 0), ACT.Identity, bias=b2_col[:, 0:1]),
                        step, "g", 0)

            def one_step(step):
                front, soft, back, ffn = (part in step.parts for part in ALL)
                if soft and step.v % 4 == 0:
                    keys(step, step.t + step.v // 4)
                if back and step.v % 4 == 1:
                    values(step, step.t + step.v // 4)
                if ffn:
                    s_part(step)
                for c in range(C):
                    if back:
                        p_copies(step, c)
                    if soft:
                        exps(step, c)
                    if back and c > 0:
                        a_part(step, c - 1)
                    if ffn:
                        relus(step, c)
                if front:
                    x_part(step, 0)
                    x_part(step, 1)
                if back:
                    a_part(step, 3)
                if soft:
                    exps(step, 4)
                if ffn:
                    g_copy(step)
                if front:
                    x_part(step, 2)
                    x_part(step, 3)
                if soft:
                    exps(step, 5)
                if front:
                    q_part(step, 0)
                    q_part(step, 1)
                if back:
                    h_part(step, 0)
                    h_part(step, 1)
                if soft:
                    exps(step, 6)
                if front:
                    q_part(step, 2)
                if back:
                    h_part(step, 2)
                    h_part(step, 3)
                if soft:
                    exps(step, 7)
                if front:
                    q_part(step, 3)

            run(act, one_step)

        @block.vector
        def _(dve):
            dve.memset(wout[:, :], 0.0).then_inc(ffn_const, 1)
            dve.memset(b2_col[:, :], 0.0).then_inc(zeroed, 1)
            dve.wait_ge(zeroed, 1)
            dve.memset(b2_col[0:DK, :], 1.0).then_inc(ffn_const, 1)
            dve.memset(w2_blocks[:, :, :], 0.0).then_inc(zeroed, 1)
            for c in range(C):
                dve.wait_ge(setup_high, c + 1)
                mm.read(dve.tensor_tensor(
                    kT_all[:, :, 1, c, :], mm.bank(SETUP, "k", c)[:, 0:B * KEYS].rearrange("p (b k) -> p b k", b=B),
                    kT_all[:, :, 0, c, :], ALU.subtract), SETUP, "k", c)
            dve.wait_ge(mask_loaded, 16)
            dve.tensor_scalar(mask_bias[:, :, :, :].rearrange("p g t k -> p g (t k)"), mask_raw, 0, MASKED,
                              ALU.is_equal, ALU.mult).then_inc(mask_ready, 1)
            for n, (name, w) in enumerate((("wq", wqT), ("wo", woT))):
                for c in range(C):
                    dve.wait_ge(setup_high, C * (n + 1) + c + 1)
                    tr.read(dve.scalar_tensor_tensor(w[:, 1, c, :], tr.bank(SETUP, name, c), W_SCALE, w[:, 0, c, :],
                                                     ALU.mult, ALU.subtract), SETUP, name, c)
            dve.wait_ge(ffn_loaded, 16 * (2 * 2 + 3 + 2 * J + 1))
            dve.wait_ge(win_high, 1)
            dve.scalar_tensor_tensor(win[:, 1, :, :], win_f[:, :, :, :].rearrange("p c a m -> p c (a m)"), W_SCALE,
                                     win[:, 0, :, :], ALU.mult, ALU.subtract).then_inc(ffn_const, 1)
            dve.tensor_scalar(bin16[:, :], bin_col[:, :], W_SCALE, None, ALU.mult).then_inc(ffn_const, 1)
            dve.tensor_scalar(w1_div[:, :], w1_col[:, :], 1.0 / W_SCALE, None, ALU.mult).then_inc(ffn_const, 1)
            dve.wait_ge(pool_const, 12)
            dve.wait_ge(zeroed, 2)
            for j in range(J):
                first = MJ * (j // 4)
                dve.tensor_scalar(w2_blocks[:, j, first:first + MJ], units[:, :], w2_col[:, j:j + 1], None, ALU.mult)\
                    .then_inc(ffn_const, 1)

            def x_statistics(step):
                g = step.group(1)
                dve.wait_ge(x_loaded[g.slot], 16 * g.lap + 16)
                for t in range(T):
                    dve.bn_stats(stats[:, 0, t, :], xr[:, g.slot, t, :]).then_inc(x_stats, 1)

            def x_means(step):
                for t in range(T):
                    dve.bn_aggr(mean_var[:, 0, t, :], stats[:, 0, t, :]).then_inc(x_mean, 1)
                dve.wait_ge(x_mean, 4 * step.group(1).n + 4)
                dve.tensor_scalar(var_eps[:, 0, :], mean_var[:, 0, :, 1], EPS, None, ALU.add).then_inc(x_eps, 1)

            def x_normal(step, t):
                g = step.group(1)
                dve.wait_ge(x_rstd, g.n + 1)
                dve.tensor_scalar(normed[:, t, :], xr[:, g.slot, t, :], mean_var[:, 0, t, 0:1], rstd[:, 0, t:t + 1],
                                  ALU.subtract, ALU.mult).then_inc(x_norm, 1)

            def x_low(step, t):
                dve.wait_ge(x_high, 4 * step.group(1).n + t + 1)
                rows = slice(P * t, P * (t + 1))
                tr.read(dve.tensor_tensor(xT[:, 1, :, rows], tr.bank(step, "xT", t).rearrange("p (c r) -> p c r", c=C),
                                          xT[:, 0, :, rows], ALU.subtract), step, "xT", t)

            def q_low(step, c):
                g = step.group(1)
                dve.wait_ge(q_high, 4 * g.n + c + 1)
                mm.read(dve.tensor_tensor(qT[:, g.parity, 1, c, :], mm.bank(step, "q", c), qT[:, g.parity, 0, c, :],
                                          ALU.subtract), step, "q", c)

            def logits_of(k):
                return lg_banks[:, k % 2, :, 0:LW].rearrange("p b (h k) -> p b h k", k=KEYS)

            def probs_of(step, k):
                return probs[:, step.group(0).parity, k // 2, 8 * KEYS * (k % 2):8 * KEYS * (k % 2 + 1)].rearrange(
                    "p (b h k) -> p b h k", b=2, h=HC)

            def maxima(step, k):
                n = HALVES * step.i + k
                dve.wait_ge(lg_ready, n + 1)
                dve.tensor_reduce(row_max[:, k % 2, :, :], logits_of(k), AX.X, ALU.max).then_inc(max_done, 1)
                dve.wait_ge(max_done, n + 1)
                dve.tensor_tensor(probs_of(step, k), logits_of(k),
                                  row_max[:, k % 2, :, :].unsqueeze(3).broadcast_to([P, 2, HC, KEYS]),
                                  ALU.subtract).then_inc(lg_free, 1)

            def sums(step, k):
                n = HALVES * step.i + k
                dve.wait_ge(exp_done, n + 1)
                dve.tensor_reduce(row_sum[:, k % 2, :, :], probs_of(step, k), AX.X, ALU.add).then_inc(sum_done, 1)
                dve.wait_ge(sum_done, n + 1)
                dve.reciprocal(row_inv[:, step.group(0).parity, k, :, :], row_sum[:, k % 2, :, :])\
                    .then_inc(inv_done, 1)

            def a_low(step, c):
                dve.wait_ge(a_high, 4 * step.group(-1).n + c + 1)
                mm.read(dve.tensor_tensor(aT[:, 1, c, :], mm.bank(step, "pv", c), aT[:, 0, c, :], ALU.subtract),
                        step, "pv", c)

            def residual(step, t):
                g = step.group(-1)
                h = xr[:, g.slot, t, :]
                mm.wait_ready(dve, step, "wo", t)
                mm.read(dve.scalar_tensor_tensor(h, mm.bank(step, "wo", t), 1.0 / W_SCALE, h, ALU.mult, ALU.add),
                        step, "wo", t)
                mm.wait_read(dve, step, "wo", t)
                dve.bn_stats(stats[:, 1, t, :], h).then_inc(h_stats, 1)

            def h_means(step):
                for t in range(T):
                    dve.bn_aggr(mean_var[:, 1, t, :], stats[:, 1, t, :]).then_inc(h_mean, 1)
                dve.wait_ge(h_mean, 4 * step.group(-1).n + 4)
                dve.tensor_scalar(var_eps[:, 1, :], mean_var[:, 1, :, 1], EPS, None, ALU.add).then_inc(h_eps, 1)

            def h_normal(step, t):
                g = step.group(-1)
                dve.wait_ge(h_rstd, g.n + 1)
                dve.tensor_scalar(normed[:, t, :], xr[:, g.slot, t, :], mean_var[:, 1, t, 0:1], rstd[:, 1, t:t + 1],
                                  ALU.subtract, ALU.mult).then_inc(h_norm, 1)

            def h_low(step, t):
                dve.wait_ge(h_high, 4 * step.group(-1).n + t + 1)
                rows = slice(P * t, P * (t + 1))
                tr.read(dve.tensor_tensor(hT[:, 1, :, rows], tr.bank(step, "hT", t).rearrange("p (c r) -> p c r", c=C),
                                          hT[:, 0, :, rows], ALU.subtract), step, "hT", t)

            def s_low(step):
                dve.wait_ge(s_high, step.group(-2).n + 1)
                low = s_parts[M:2 * M, :]
                mm.read(dve.scalar_tensor_tensor(low, mm.bank(step, "s", 0)[M:2 * M, :], bin16[M:2 * M, 0:1], low,
                                                 ALU.add, ALU.subtract), step, "s", 0)

            def output(step, t):
                h = xr[:, step.group(-2).slot, t, :]
                mm.wait_ready(dve, step, "out", t)
                mm.read(dve.tensor_tensor(h, mm.bank(step, "out", t), h, ALU.add), step, "out", t)

            def one_step(step):
                front, soft, back, ffn = (part in step.parts for part in ALL)
                if soft:
                    maxima(step, 0)
                if ffn:
                    s_low(step)
                if front:
                    x_statistics(step)
                    dve.wait_ge(x_stats, 4 * step.group(1).n + 4)
                if soft:
                    maxima(step, 1)
                if front:
                    x_means(step)
                for c in range(1, C):
                    if soft and c > 1:
                        maxima(step, c)
                    if soft:
                        sums(step, c - 1)
                    if back:
                        a_low(step, c - 1)
                    if front and c > 1:
                        x_normal(step, 2 * c - 4)
                        x_normal(step, 2 * c - 3)
                if soft:
                    maxima(step, 4)
                if front:
                    x_low(step, 0)
                    x_low(step, 1)
                if back:
                    a_low(step, 3)
                if soft:
                    sums(step, 3)
                if front:
                    x_low(step, 2)
                    x_low(step, 3)
                if soft:
                    sums(step, 4)
                if back:
                    residual(step, 0)
                    residual(step, 1)
                if ffn:
                    output(step, 0)
                if back:
                    residual(step, 2)
                if ffn:
                    output(step, 1)
                if back:
                    residual(step, 3)
                    dve.wait_ge(h_stats, 4 * step.group(-1).n + 4)
                if ffn:
                    output(step, 2)
                if back:
                    h_means(step)
                if ffn:
                    output(step, 3)
                if soft:
                    maxima(step, 5)
                if back:
                    for t in range(T):
                        h_normal(step, t)
                if front:
                    q_low(step, 0)
                    q_low(step, 1)
                if back:
                    h_low(step, 0)
                    h_low(step, 1)
                if soft:
                    maxima(step, 6)
                    sums(step, 5)
                if front:
                    q_low(step, 2)
                if back:
                    h_low(step, 2)
                    h_low(step, 3)
                if soft:
                    maxima(step, 7)
                    sums(step, 6)
                if front:
                    q_low(step, 3)
                if soft:
                    sums(step, 7)

            run(dve, one_step)

        @block.tensor
        def _(pe):
            pe.wait_ge(pool_const, 4)

            pe.wait_ge(ctx_loaded, 16)
            for c in range(C):
                tr.wait_free(pe, SETUP, "ctxT", c)
                bank = tr.bank(SETUP, "ctxT", c)
                for b in range(B):
                    last = pe.transpose(bank[:, KEYS * b:KEYS * (b + 1)], ctx_raw[:, b, P * c:P * (c + 1)],
                                        ident[0:KEYS, 0:KEYS])
                last.then_inc(tr_ready, 1)

            def weight(n, name):
                pe.wait_ge(w_loaded[n], 16)
                for c in range(C):
                    tr.wait_free(pe, SETUP, name, c)
                    bank = tr.bank(SETUP, name, c)
                    for o in range(C):
                        last = pe.transpose(bank[:, P * o:P * (o + 1)], w_raw[:, n, o, P * c:P * (c + 1)], ident[:, :])
                    last.then_inc(tr_ready, 1)

            weight(0, "wk")
            for c in range(C):
                tr.wait_read(pe, SETUP, "wk", c)
            for o in range(C):
                mm.wait_free(pe, SETUP, "k", o)
                for c in range(C):
                    last = pe.matmul(mm.bank(SETUP, "k", o)[:, 0:B * KEYS], wkT[:, c, P * o:P * (o + 1)],
                                     ctxT[:, c, :], start=(c == 0), stop=(c == C - 1))
                last.then_inc(mm_ready, 1)
            weight(1, "wv")
            for c in range(C):
                tr.wait_read(pe, SETUP, "wv", c)
            for b in range(B):
                mm.wait_free(pe, SETUP, "v", b)
                for c in range(C):
                    last = pe.matmul(mm.bank(SETUP, "v", b)[0:KEYS, :], ctxT[:, c, KEYS * b:KEYS * (b + 1)],
                                     wvT[:, c, :], start=(c == 0), stop=(c == C - 1))
                last.then_inc(mm_ready, 1)
            weight(2, "wq")
            weight(3, "wo")

            def three_passes(bank, stationary, moving, chunks):
                passes = [(c, a, b) for c in range(chunks) for a, b in ((0, 0), (0, 1), (1, 0))]
                for n, (c, a, b) in enumerate(passes):
                    last = pe.matmul(bank, stationary(a, c), moving(b, c), start=(n == 0),
                                     stop=(n == len(passes) - 1))
                return last

            def x_transpose(step, t):
                g = step.group(1)
                tr.wait_free(pe, step, "xT", t)
                pe.wait_ge(x_norm, 4 * g.n + t + 1)
                for c in range(C):
                    last = pe.transpose(tr.bank(step, "xT", t)[:, P * c:P * (c + 1)], normed[:, t, P * c:P * (c + 1)],
                                        ident[:, :])
                last.then_inc(tr_ready, 1)

            def q(step, o):
                if o == 0:
                    for t in (T - 2, T - 1):
                        tr.wait_read(pe, step, "xT", t)
                    if step.first(-1):
                        for c in (C - 2, C - 1):
                            tr.wait_read(pe, SETUP, "wq", c)
                mm.wait_free(pe, step, "q", o)
                three_passes(mm.bank(step, "q", o), lambda a, c: wqT[:, a, c, P * o:P * (o + 1)],
                             lambda b, c: xT[:, b, c, :], C).then_inc(mm_ready, 1)

            def logits(step, k):
                n = HALVES * step.i + k
                g = step.group(0)
                t, u = k // 2, k % 2
                if k < 2:
                    mm.wait_all_read(pe, step, but=1 - k)
                if k == 0 and step.first(0):
                    pe.wait_ge(mask_ready, 1)
                if k == 0 and step.v % 4 == 0:
                    pe.wait_ge(k_ready, 16 * HC * (step.t + step.v // 4 + 1))
                if not (isinstance(n, int) and n < 2):
                    pe.wait_ge(lg_free, n - 1)
                rows = slice(P * t, P * (t + 1))
                for b in range(2):
                    c = 2 * u + b
                    bank = lg_banks[:, k % 2, b, 0:LW]
                    for m, (qp, kp) in enumerate(((0, 0), (0, 1), (1, 0))):
                        pe.matmul(bank, qT[:, g.parity, qp, c, rows], k_blocks[:, kp, c, :], start=(m == 0), stop=False)
                    last = pe.matmul(bank.rearrange("p (h k) -> p h k", k=KEYS), ident_bf[:, :],
                                     mask_bias[:, g.slot, t, :].unsqueeze(1).broadcast_to([P, HC, KEYS]),
                                     start=False, stop=True)
                last.then_inc(lg_ready, 1)

            def p_transposes(step, c):
                g = step.group(-1)
                if c == 0:
                    pe.wait_ge(probs_ready, HALVES * g.n + HALVES)
                for h in range(HC * c, HC * (c + 1)):
                    tr.wait_free(pe, step, "pT", h)
                    for t in range(T):
                        last = pe.transpose(tr.bank(step, "pT", h)[0:KEYS, P * t:P * (t + 1)],
                                            probs[:, g.parity, t, KEYS * h:KEYS * (h + 1)], ident[:, :])
                    last.then_inc(tr_ready, 1)

            def pv(step, c):
                if c == 0 and step.v % 4 == 1:
                    pe.wait_ge(v_ready, 16 * (step.t + step.v // 4 + 1))
                for h in (2, 3):
                    tr.wait_read(pe, step, "pT", HC * c + h)
                mm.wait_free(pe, step, "pv", c)
                for h in range(HC):
                    last = pe.matmul(mm.bank(step, "pv", c)[DK * h:DK * (h + 1), :],
                                     v_now[:, DK * (HC * c + h):DK * (HC * c + h + 1)], pT[0:KEYS, (HC * c + h) % 8, :],
                                     start=True, stop=True)
                last.then_inc(mm_ready, 1)

            def wo(step, t):
                if t == 0:
                    for c in (C - 2, C - 1):
                        mm.wait_read(pe, step, "pv", c)
                mm.wait_free(pe, step, "wo", t)
                three_passes(mm.bank(step, "wo", t), lambda a, c: aT[:, a, c, P * t:P * (t + 1)],
                             lambda b, c: woT[:, b, c, :], C).then_inc(mm_ready, 1)

            def h_transpose(step, t):
                tr.wait_free(pe, step, "hT", t)
                pe.wait_ge(h_norm, 4 * step.group(-1).n + t + 1)
                for c in range(C):
                    last = pe.transpose(tr.bank(step, "hT", t)[:, P * c:P * (c + 1)], normed[:, t, P * c:P * (c + 1)],
                                        ident[:, :])
                last.then_inc(tr_ready, 1)

            def ffn_in(step):
                tr.wait_all_read(pe, step)
                if step.first(FIRST_FULL):
                    pe.wait_ge(ffn_const, 5 + J)
                mm.wait_free(pe, step, "s", 0)
                three_passes(mm.bank(step, "s", 0), lambda a, c: win[:, a, c, :], lambda b, c: hT[:, b, c, :], C)\
                    .then_inc(mm_ready, 1)

            def ffn_pre(step, j):
                if j == 0:
                    mm.wait_read(pe, step, "s", 0)
                tr.wait_free(pe, step, "pre", j)
                pe.matmul(tr.bank(step, "pre", j), spread[:, j, :], s_parts[:, :], start=True, stop=True)\
                    .then_inc(tr_ready, 1)

            def ffn_g(step, j):
                if j == 0:
                    mm.wait_free(pe, step, "g", 0)
                tr.wait_read(pe, step, "pre", j)
                group = DK * (j % 4)
                last = pe.matmul(mm.bank(step, "g", 0)[group:group + DK, :], w2_blocks[:, j, :], inner[:, j, :],
                                 start=(j < 4), stop=(j >= 4))
                if j == J - 1:
                    last.then_inc(mm_ready, 1)

            def ffn_out(step, t):
                if t == 0:
                    mm.wait_read(pe, step, "g", 0)
                mm.wait_free(pe, step, "out", t)
                pe.matmul(mm.bank(step, "out", t), gT[:, P * t:P * (t + 1)], wout[:, :], start=True, stop=True)\
                    .then_inc(mm_ready, 1)

            def one_step(step):
                front, soft, back, ffn = (part in step.parts for part in ALL)
                if soft:
                    logits(step, 0)
                if ffn:
                    ffn_in(step)
                for c in range(C):
                    if c > 0 and soft:
                        logits(step, c)
                    if back:
                        p_transposes(step, c)
                        if c > 0:
                            pv(step, c - 1)
                    if ffn:
                        ffn_pre(step, 2 * c)
                        ffn_pre(step, 2 * c + 1)
                if soft:
                    logits(step, 4)
                if front:
                    x_transpose(step, 0)
                    x_transpose(step, 1)
                if back:
                    pv(step, 3)
                if ffn:
                    for j in range(J):
                        ffn_g(step, j)
                if front:
                    x_transpose(step, 2)
                    x_transpose(step, 3)
                if back:
                    wo(step, 0)
                    wo(step, 1)
                if ffn:
                    ffn_out(step, 0)
                if back:
                    wo(step, 2)
                if ffn:
                    ffn_out(step, 1)
                if back:
                    wo(step, 3)
                if ffn:
                    ffn_out(step, 2)
                    ffn_out(step, 3)
                if soft:
                    logits(step, 5)
                if front:
                    q(step, 0)
                    q(step, 1)
                if back:
                    h_transpose(step, 0)
                    h_transpose(step, 1)
                if soft:
                    logits(step, 6)
                if front:
                    q(step, 2)
                if back:
                    h_transpose(step, 2)
                    h_transpose(step, 3)
                if soft:
                    logits(step, 7)
                if front:
                    q(step, 3)
                if step.first(-1):
                    pe.wait_ge(ffn_const, 5 + J)
                    pe.wait_ge(pool_const, 12)
                    for c in (C - 2, C - 1):
                        tr.wait_read(pe, SETUP, "wo", c)

            run(pe, one_step)


_INS = ['x', 'ctx_1024', 'mask_1x1xSxS2_ik0', 'L0_xattn_Wq', 'L0_xattn_Wk', 'L0_xattn_Wv', 'L0_xattn_Wo',
        'L0_ffn_Win', 'L0_ffn_bin_', 'L0_ffn_W1', 'L0_ffn_b1', 'L0_ffn_W2', 'L0_ffn_b2', 'L0_ffn_Wout', 'L0_ffn_bout']


def kernel(**inputs):
    import numpy as _np
    import concourse.bacc as _bacc
    from concourse import mybir as _mybir
    from concourse.bass_utils import run_bass_kernel_spmd as _run

    nc = _bacc.Bacc("TRN2", target_bir_lowering=False, num_devices=1)
    arrays, args = {}, []
    for name in _INS:
        a = _np.ascontiguousarray(inputs[name])
        arrays[f"in_{name}"] = a
        args.append(nc.dram_tensor(f"in_{name}", a.shape, _mybir.dt.from_np(a.dtype), kind="ExternalInput").ap())
    args.append(nc.dram_tensor("out_x", (B, S, D), _mybir.dt.float32, kind="ExternalOutput").ap())
    build(nc, *args)
    r = _run(nc, [arrays], core_ids=[0])
    return r.results[0]["out_x"]
```

```python
from contextlib import ExitStack

import concourse.bass as bass
from concourse import mybir

F32 = mybir.dt.float32
F16 = mybir.dt.float16
BF16 = mybir.dt.bfloat16
I32 = mybir.dt.int32
ALU = mybir.AluOpType
ACT = mybir.ActivationFunctionType
AX = mybir.AxisListType

P = 128
D = 512
C = D // P
B = 4
S = 2048
T = 4
ROWS = T * P
GROUPS = B * S // ROWS
PER_BATCH = GROUPS // B
KEYS = 77
HEADS = 16
DK = D // HEADS
HC = P // DK
LW = HC * KEYS
HALVES = 2 * T
M = 64
INNER = 16
J = M * INNER // P
MJ = M // J
W_SCALE = 16.0
MASKED = -(2.0 ** 100)
EPS = 1e-5

SETUP, AHEAD, FRONT, SOFT, BACK, FFN, LATE = "setup", "ahead", "front", "soft", "back", "ffn", "late"
ALL = (AHEAD, FRONT, SOFT, BACK, FFN)
FIRST_FULL = 2
LOOPED = 4 * (GROUPS // 4 - 1)

TR_SETUP = ([("ctxT", c) for c in range(C)] + [("inner", 0), ("inner", 1)]
            + [(w, c) for w in ("wkT", "wqT") for c in range(C)])
TR_ORDER = (
    [(FRONT, "xT", k) for k in range(0, 2)] + [(BACK, "pT", k) for k in range(0, 2)] + [(FFN, "pre", 0)]
    + [(BACK, "pT", 2)] + [(FFN, "pre", 1)] + [(BACK, "pT", k) for k in range(3, 5)]
    + [(FFN, "pre", k) for k in range(2, 4)] + [(BACK, "pT", 5)] + [(FFN, "pre", k) for k in range(4, 6)]
    + [(BACK, "pT", 6)] + [(FFN, "pre", k) for k in range(6, 8)] + [(BACK, "pT", 7)] + [(FRONT, "xT", 2)]
    + [(LATE, "wvT", k) for k in range(0, 4)] + [(BACK, "pT", k) for k in range(8, 12)] + [(FRONT, "xT", 3)]
    + [(BACK, "pT", k) for k in range(12, 15)] + [(LATE, "woT", k) for k in range(0, 2)] + [(BACK, "pT", 15)]
    + [(LATE, "woT", k) for k in range(2, 4)] + [(BACK, "hT", k) for k in range(0, 4)]
)
MM_SETUP = [("k", c) for c in range(C)]
MM_ORDER = (
    [(FFN, "s", 0)] + [(BACK, "pv", 0)] + [(FFN, "g", 0)] + [(BACK, "pv", 1)]
    + [(FFN, "out", k) for k in range(0, 3)] + [(LATE, "v", k) for k in range(0, 2)] + [(FFN, "out", 3)]
    + [(BACK, "pv", 2)] + [(FRONT, "q", 0)] + [(LATE, "v", k) for k in range(2, 4)] + [(FRONT, "q", 1)]
    + [(BACK, "pv", 3)] + [(FRONT, "q", 2)] + [(BACK, "wo", k) for k in range(0, 4)] + [(FRONT, "q", 3)]
)


def parts_of(i):
    parts = tuple(part for part, ahead in zip(ALL, (2, 1, 0, -1, -2)) if 0 <= i + ahead < GROUPS)
    return parts + (LATE,) if i == 0 else parts


class Step:

    def __init__(self, t, v):
        self.t, self.v = t, v
        self.i = 4 * t + v
        self.parts = parts_of(self.i) if isinstance(self.i, int) else ALL

    def first(self, i):
        return isinstance(self.i, int) and self.i == i

    def group(self, ahead):
        return Group(self.t, self.v + ahead)


class Group:

    def __init__(self, t, v):
        self.n, self.slot, self.lap, self.parity = 4 * t + v, v % 4, t + v // 4, v % 2


def half_of(step, k):
    group = step.group(0) if k >= 0 else step.group(-1)
    return group, k % HALVES, HALVES * step.i + k


class Ring:

    def __init__(self, setup, order, tensor, ready, free):
        self.setup, self.order, self.tensor, self.ready, self.free = setup, order, tensor, ready, free

    def half(self, step):
        def uses(i):
            return sum(part in parts_of(i) for part, _, _ in self.order)

        if step is SETUP:
            return 0
        if isinstance(step.i, int):
            return (len(self.setup) + sum(uses(i) for i in range(-1, step.i))) // 2
        before = (len(self.setup) + sum(uses(i) for i in range(-1, FIRST_FULL))) // 2
        return before + (step.i - FIRST_FULL) * (uses(FIRST_FULL) // 2)

    def place(self, step, name, k):
        if step is SETUP:
            return self.setup.index((name, k))
        return [(n, m) for part, n, m in self.order if part in step.parts].index((name, k))

    def bank(self, step, name, k):
        return self.tensor[:, self.place(step, name, k) % 2, :]

    def wait_free(self, eng, step, name, k):
        place = self.place(step, name, k)
        value = self.half(step) + place // 2
        if not (isinstance(value, int) and value < 1):
            eng.wait_ge(self.free[place % 2], value)

    def wait_ready(self, eng, step, name, k):
        eng.wait_ge(self.ready, 2 * self.half(step) + self.place(step, name, k) + 1)

    def wait_read(self, eng, step, name, k):
        place = self.place(step, name, k)
        eng.wait_ge(self.free[place % 2], self.half(step) + place // 2 + 1)

    def wait_all_read(self, eng, step):
        for b in range(2):
            eng.wait_ge(self.free[b], self.half(step))

    def read(self, instruction, step, name, k):
        instruction.then_inc(self.free[self.place(step, name, k) % 2], 1)


def build(nc, x, ctx_in, mask, Wq, Wk, Wv, Wo, Win, bin_, W1, b1, W2, b2, Wout, bout, out):
    stack = ExitStack()
    with stack:
        def sb(name, shape, dt):
            return stack.enter_context(nc.sbuf_tensor(name, shape, dt))

        def sem(name):
            return stack.enter_context(nc.semaphore(name))

        tr_banks = stack.enter_context(nc.psum_tensor("tr_banks", [P, 2, D], F32))
        mm_banks = stack.enter_context(nc.psum_tensor("mm_banks", [P, 2, D], F32))
        lg_banks = stack.enter_context(nc.psum_tensor("lg_banks", [P, 2, 2, 512], F32))

        ident = sb("ident", [P, P], F32)
        wqT = sb("wqT", [P, 2, C, D], F16)
        woT = sb("woT", [P, 2, C, D], F16)
        win = sb("win", [P, 2, C, 2 * M], F16)
        kT_all = sb("kT_all", [P, B, 2, C, KEYS], F16)
        k_blocks = sb("k_blocks", [P, 2, 2, C, LW], F16)
        v_all = sb("v_all", [KEYS, B, D], F32)
        v_now = sb("v_now", [KEYS, D], F32)
        mask_bias = sb("mask_bias", [P, PER_BATCH, T, KEYS], BF16)
        spread = sb("spread", [P, J, P], F16)
        inner_cols = sb("inner_cols", [P, 3, J], F32)
        w1_div = sb("w1_div", [P, J], F32)
        units = sb("units", [P, MJ], F32)
        w2_blocks = sb("w2_blocks", [P, J, DK], F32)
        bin_col = sb("bin_col", [P, 1], F32)
        bin16 = sb("bin16", [P, 1], F32)
        b2_col = sb("b2_col", [P, 1], F32)
        wout = sb("wout", [P, D], F16)
        bout_rows = sb("bout_rows", [P, D], F32)
        neg_half = sb("neg_half", [P, T], F32)

        xr = sb("xr", [P, 4, T, D], F32)
        normed = sb("normed", [P, T, D], F32)
        xT = sb("xT", [P, 2, C, ROWS], F16)
        hT = sb("hT", [P, 2, C, ROWS], F16)
        qT = sb("qT", [P, 2, 2, C, ROWS], F16)
        probs = sb("probs", [P, 2, T, HEADS * KEYS], F32)
        pT = sb("pT", [P, 8, ROWS], F32)
        aT = sb("aT", [P, 2, C, ROWS], F16)
        s_parts = sb("s_parts", [P, ROWS], F16)
        inner = sb("inner", [P, J, ROWS], F32)
        gT = sb("gT", [P, 2, ROWS], F16)
        stats = sb("stats", [P, 2, T, 6], F32)
        mean_var = sb("mean_var", [P, 2, T, 2], F32)
        var_eps = sb("var_eps", [P, 2, T], F32)
        rstd = sb("rstd", [P, 2, T], F32)
        minus_mean = sb("minus_mean", [P, T], F32)
        shift = sb("shift", [P, T], F32)
        row_max = sb("row_max", [P, 2, HALVES, 2, HC], F32)
        row_sum = sb("row_sum", [P, 2, 2, HC], F32)
        row_inv = sb("row_inv", [P, 2, HALVES, 2, HC], F32)

        w_raw = [probs[:, n // 2, :, :].rearrange("p t n -> p (t n)")[:, C * D * (n % 2):C * D * (n % 2 + 1)].rearrange(
            "p (c n) -> p c n", c=C) for n in range(4)]
        wkT = pT[:, 0:4, :]
        wvT = pT[:, 4:8, :]
        win_f = inner[:, 0, :].rearrange("p (c a m) -> p c a m", c=C, a=2)
        in_rows = [inner[0:2 * J, 1, 0:P], inner[0:J, 1, P:2 * P]]
        wout_f = inner[0:M, 2, :]
        wout_parts = inner[0:M, 3, :].bitcast(F16).rearrange("m (a d) -> m a d", a=2)
        ctxT = inner[:, 4:4 + C, 0:B * KEYS]
        ctx_raw = xr[0:KEYS, 3, :, :]
        mask_raw = normed[:, :, 0:T * KEYS].bitcast(I32)

        ctx_loaded = sem("ctx_loaded")
        w_loaded = [sem(f"w_loaded_{w}") for w in ("k", "q", "v", "o")]
        mask_loaded = sem("mask_loaded")
        ffn_loaded = sem("ffn_loaded")
        bout_loaded = sem("bout_loaded")
        wout_loaded = sem("wout_loaded")
        wout_high = sem("wout_high")
        wout_low = sem("wout_low")
        wout_placed = sem("wout_placed")
        rows_loaded = sem("rows_loaded")
        x_loaded = [[sem(f"x_loaded_{s}_{h}") for h in range(2)] for s in range(4)]
        out_stored = [[sem(f"out_stored_{s}_{h}") for h in range(2)] for s in range(4)]
        pool_const = sem("pool_const")
        ffn_const = sem("ffn_const")
        mask_ready = sem("mask_ready")
        zeroed = sem("zeroed")
        tr_ready = sem("tr_ready")
        mm_ready = sem("mm_ready")
        lg_ready = sem("lg_ready")
        tr_free = [sem("tr_free_0"), sem("tr_free_1")]
        mm_free = [sem("mm_free_0"), sem("mm_free_1")]
        lg_free = sem("lg_free")
        setup_high = sem("setup_high")
        win_high = sem("win_high")
        x_stats = sem("x_stats")
        x_mean = sem("x_mean")
        x_eps = sem("x_eps")
        x_rstd = sem("x_rstd")
        x_minus = sem("x_minus")
        x_shift = sem("x_shift")
        x_norm = sem("x_norm")
        x_high = sem("x_high")
        q_high = sem("q_high")
        max_done = sem("max_done")
        shifted = sem("shifted")
        exp_done = sem("exp_done")
        sum_done = sem("sum_done")
        inv_done = sem("inv_done")
        probs_ready = sem("probs_ready")
        k_ready = [sem("k_ready_0"), sem("k_ready_1")]
        v_ready = sem("v_ready")
        a_high = sem("a_high")
        h_stats = sem("h_stats")
        h_mean = sem("h_mean")
        h_eps = sem("h_eps")
        h_rstd = sem("h_rstd")
        h_norm = sem("h_norm")
        h_high = sem("h_high")
        s_high = sem("s_high")
        g_high = sem("g_high")
        bout_added = sem("bout_added")

        tr = Ring(TR_SETUP, TR_ORDER, tr_banks, tr_ready, tr_free)
        mm = Ring(MM_SETUP, MM_ORDER, mm_banks, mm_ready, mm_free)

        x_rows = x.rearrange("b (g p t) d -> (b g) p t d", p=P, t=T)
        out_rows = out.rearrange("b (g p t) d -> (b g) p t d", p=P, t=T)

        def run(eng, one_step):
            for i in range(-2, FIRST_FULL):
                one_step(Step(0, i))
            with eng.Fori(0, LOOPED // 4, 1) as t:
                for v in range(FIRST_FULL, FIRST_FULL + 4):
                    one_step(Step(t, v))
            for i in range(FIRST_FULL + LOOPED, GROUPS + 2):
                one_step(Step(0, i))

        block = stack.enter_context(nc.Block())

        @block.sync
        def _(sp):
            def load(g, halves=(0, 1)):
                for half in halves:
                    tiles = slice(2 * half, 2 * half + 2)
                    sp.dma_start(xr[:, g.slot, tiles, :], x_rows[g.n][:, tiles, :]).then_inc(x_loaded[g.slot][half], 16)

            sp.dma_start(ctx_raw, ctx_in.rearrange("b k d -> k b d")).then_inc(ctx_loaded, 16)
            sp.dma_start(w_raw[0], Wk.rearrange("(c p) n -> p c n", p=P)).then_inc(w_loaded[0], 16)
            load(Group(0, 0))
            sp.dma_start(w_raw[1], Wq.rearrange("(c p) n -> p c n", p=P)).then_inc(w_loaded[1], 16)
            load(Group(0, 1))
            for n, w in ((2, Wv), (3, Wo)):
                sp.dma_start(w_raw[n], w.rearrange("(c p) n -> p c n", p=P)).then_inc(w_loaded[n], 16)
            load(Group(0, 2))

            def keys(buffer, batch):
                for j in range(HC):
                    rows = slice(DK * j, DK * (j + 1))
                    sp.dma_start(
                        k_blocks[rows, buffer, :, :, KEYS * j:KEYS * (j + 1)].rearrange("p a c k -> p (a c) k"),
                        kT_all[rows, bass.ds(batch, 1), :, :, :].rearrange("p b a c k -> p (b a c) k"))\
                        .then_inc(k_ready[buffer], 16)

            sp.wait_ge(pool_const, 4)
            for c in (C - 2, C - 1):
                mm.wait_read(sp, SETUP, "k", c)
            for buffer in range(2):
                keys(buffer, 0)
            tr.wait_ready(sp, SETUP, "ctxT", C - 1)
            load(Group(0, 3))

            for twice in range(2):
                sp.dma_start(win_f[:, :, twice, :], Win.rearrange("(c p) m -> p c m", p=P)).then_inc(ffn_loaded, 16)
                sp.dma_start(bin_col[M * twice:M * (twice + 1), :], bin_.rearrange("(m a) -> m a", a=1))\
                    .then_inc(ffn_loaded, 16)
            sp.dma_start(wout_f, Wout).then_inc(wout_loaded, 16)
            sp.dma_start(bout_rows[:, :], bout.rearrange("(a d) -> a d", a=1).broadcast_to([P, D]))\
                .then_inc(bout_loaded, 16)

            def unit_rows(j, twice):
                first = DK * (j % 4) + MJ * (j // 4) + DK // 2 * twice
                return slice(first, first + MJ)

            for j in range(J):
                for twice in range(2):
                    sp.dma_start(b2_col[unit_rows(j, twice), :], b2[MJ * j:MJ * (j + 1)].rearrange(
                        "(m a) -> m a", a=1)).then_inc(ffn_loaded, 16)

            sp.wait_ge(wout_high, 1)
            sp.wait_ge(wout_low, 1)
            for j in range(J):
                for part in range(2):
                    sp.dma_start(wout[unit_rows(j, part), :], wout_parts[MJ * j:MJ * (j + 1), part, :])\
                        .then_inc(wout_placed, 16)

            def store(step, half):
                g = step.group(-2)
                mm.wait_read(sp, step, "out", 2 * half + 1)
                tiles = slice(2 * half, 2 * half + 2)
                sp.dma_start(out_rows[g.n][:, tiles, :], xr[:, g.slot, tiles, :]).then_inc(out_stored[g.slot][half], 16)

            with sp.Fori(0, LOOPED // 4, 1) as t:
                for v in range(FIRST_FULL, FIRST_FULL + 4):
                    step = Step(t, v)
                    if v % 2 == 0:
                        sp.wait_ge(lg_ready, HALVES * step.i)
                        keys(0 if v % 4 == 2 else 1, t + 1)
                    for half in range(2):
                        store(step, half)
                        sp.wait_ge(out_stored[step.group(2).slot][half], 16 * step.group(2).lap)
                        load(step.group(2), (half,))
            for i in range(FIRST_FULL + LOOPED, GROUPS + 2):
                for half in range(2):
                    store(Step(0, i), half)
            for s in range(4):
                for half in range(2):
                    sp.wait_ge(out_stored[s][half], 16 * (GROUPS // 4))

        @block.gpsimd
        def _(pool):
            pool.memset(ident[:, :], 0.0).then_inc(pool_const, 1)
            pool.wait_ge(pool_const, 1)
            pool.affine_select(out=ident[:, :], in_=ident[:, :], compare_op=ALU.not_equal, fill=1.0, base=0,
                               pattern=[[-1, P]], channel_multiplier=1).then_inc(pool_const, 1)
            pool.memset(neg_half[:, :], -0.5).then_inc(pool_const, 1)
            pool.memset(k_blocks[:, :, :, :, :], 0.0).then_inc(pool_const, 1)
            pool.memset(spread[:, :, :], 0.0).then_inc(pool_const, 1)
            pool.memset(units[:, :], 1.0).then_inc(pool_const, 1)
            for n, first in enumerate((0, -M)):
                pool.wait_ge(pool_const, 6 + n)
                v = spread[:, :, :].rearrange("p j (i n) -> p j i n", n=INNER)
                pool.affine_select(out=v, in_=v, compare_op=ALU.not_equal, fill=1.0, base=first,
                                   pattern=[[-MJ, J], [-1, MJ], [0, INNER]], channel_multiplier=1)\
                    .then_inc(pool_const, 1)
            pool.wait_ge(pool_const, 8)
            pool.affine_select(out=units[:, :], in_=units[:, :], compare_op=ALU.is_ge, fill=0.0, base=0,
                               pattern=[[-INNER, MJ]], channel_multiplier=1).then_inc(pool_const, 1)
            pool.wait_ge(pool_const, 9)
            pool.affine_select(out=units[:, :], in_=units[:, :], compare_op=ALU.is_ge, fill=0.0, base=INNER - 1,
                               pattern=[[INNER, MJ]], channel_multiplier=-1).then_inc(pool_const, 1)

            def front_rstd(step):
                pool.wait_ge(x_eps, step.i + 3)
                pool.tensor_tensor(rstd[:, 0, :], var_eps[:, 0, :], neg_half[:, :], ALU.pow).then_inc(x_rstd, 1)
                pool.wait_ge(x_rstd, step.i + 3)
                pool.wait_ge(x_minus, step.i + 3)
                pool.tensor_tensor(shift[:, :], minus_mean[:, :], rstd[:, 0, :], ALU.mult).then_inc(x_shift, 1)

            def back_rstd(step, pair):
                n = 2 * (step.i - 1) + pair
                tiles = slice(2 * pair, 2 * pair + 2)
                pool.wait_ge(h_eps, n + 1)
                pool.tensor_tensor(rstd[:, 1, tiles], var_eps[:, 1, tiles], neg_half[:, tiles], ALU.pow)\
                    .then_inc(h_rstd, 1)

            def add_bout(step, t):
                g = step.group(-1)
                if step.first(1) and t == 0:
                    pool.wait_ge(bout_loaded, 16)
                pool.wait_ge(h_norm, 4 * g.n + t + 1)
                h = xr[:, g.slot, t, :]
                pool.tensor_tensor(h, h, bout_rows[:, :], ALU.add).then_inc(bout_added, 1)

            def block_of(g, k):
                return probs[:, g.parity, k // 2, 8 * KEYS * (k % 2):8 * KEYS * (k % 2 + 1)].rearrange(
                    "p (b h k) -> p b h k", b=2, h=HC)

            def subtract_max(step, k):
                g, k, n = half_of(step, k)
                pool.wait_ge(max_done, n + 1)
                top = row_max[:, g.parity, k, :, :].unsqueeze(3).broadcast_to([P, 2, HC, KEYS])
                pool.tensor_tensor(block_of(g, k), block_of(g, k), top, ALU.subtract).then_inc(shifted, 1)

            def divide(step, k):
                g, k, n = half_of(step, k)
                pool.wait_ge(inv_done, n + 1)
                inv = row_inv[:, g.parity, k, :, :].unsqueeze(3).broadcast_to([P, 2, HC, KEYS])
                pool.tensor_tensor(block_of(g, k), block_of(g, k), inv, ALU.mult).then_inc(probs_ready, 1)

            def one_step(step):
                ahead, front, soft, back, ffn = (part in step.parts for part in ALL)
                if back:
                    subtract_max(step, -1)
                if soft:
                    subtract_max(step, 0)
                    subtract_max(step, 1)
                if back:
                    divide(step, -1)
                if soft:
                    divide(step, 0)
                    subtract_max(step, 2)
                    subtract_max(step, 3)
                    subtract_max(step, 4)
                    subtract_max(step, 5)
                    divide(step, 1)
                    divide(step, 2)
                    subtract_max(step, 6)
                    divide(step, 3)
                if back:
                    back_rstd(step, 0)
                if ahead:
                    front_rstd(step)
                if back:
                    add_bout(step, 0)
                if soft:
                    divide(step, 4)
                if back:
                    back_rstd(step, 1)
                    add_bout(step, 1)
                    add_bout(step, 2)
                if soft:
                    divide(step, 5)
                if back:
                    add_bout(step, 3)
                if soft:
                    divide(step, 6)

            run(pool, one_step)

        @block.scalar
        def _(act):
            for rows, w in ((in_rows[0][0:J, :], W1), (in_rows[0][J:2 * J, :], b1), (in_rows[1], W2)):
                act.dma_start(rows, w.rearrange("(j i) n -> j (i n)", i=MJ)).then_inc(rows_loaded, 16)
            act.dma_start(mask_raw, mask[0, 0].rearrange("(g p t) k -> p g (t k)", p=P, t=T)).then_inc(mask_loaded, 16)
            for c in range(C):
                tr.wait_ready(act, SETUP, "ctxT", c)
                tr.read(act.activation(ctxT[:, c, :], tr.bank(SETUP, "ctxT", c)[:, 0:B * KEYS], ACT.Copy),
                        SETUP, "ctxT", c)
            for n in range(2):
                tr.wait_ready(act, SETUP, "inner", n)
                cols = inner_cols[:, 2 * n:2 + n, :].rearrange("p w j -> p (w j)")
                tr.read(act.activation(cols, tr.bank(SETUP, "inner", n)[:, 0:(2 - n) * J], ACT.Copy),
                        SETUP, "inner", n)
            for c in range(C):
                tr.wait_ready(act, SETUP, "wkT", c)
                tr.read(act.activation(wkT[:, c, :], tr.bank(SETUP, "wkT", c), ACT.Copy), SETUP, "wkT", c)
            for c in range(C):
                mm.wait_ready(act, SETUP, "k", c)
                act.activation(kT_all[:, :, 0, c, :], mm.bank(SETUP, "k", c)[:, 0:B * KEYS].rearrange(
                    "p (b k) -> p b k", b=B), ACT.Copy).then_inc(setup_high, 1)
            for c in range(C):
                tr.wait_ready(act, SETUP, "wqT", c)
                act.activation(wqT[:, 0, c, :], tr.bank(SETUP, "wqT", c), ACT.Copy, scale=W_SCALE)\
                    .then_inc(setup_high, 1)

            def wv_copy(step, c):
                tr.wait_ready(act, step, "wvT", c)
                tr.read(act.activation(wvT[:, c, :], tr.bank(step, "wvT", c), ACT.Copy), step, "wvT", c)

            def v_copy(step, b):
                mm.wait_ready(act, step, "v", b)
                mm.read(act.activation(v_all[:, b, :], mm.bank(step, "v", b)[0:KEYS, :], ACT.Copy), step, "v", b)

            def wo_part(step, c):
                tr.wait_ready(act, step, "woT", c)
                act.activation(woT[:, 0, c, :], tr.bank(step, "woT", c), ACT.Copy, scale=W_SCALE)\
                    .then_inc(setup_high, 1)

            def ffn_weights():
                act.wait_ge(wout_loaded, 16)
                act.activation(wout_parts[:, 0, :], wout_f, ACT.Copy, scale=W_SCALE).then_inc(wout_high, 1)
                act.wait_ge(ffn_loaded, 16 * (2 * 2 + 2 * J))
                act.activation(win[:, 0, :, :], win_f[:, :, :, :].rearrange("p c a m -> p c (a m)"), ACT.Copy,
                               scale=W_SCALE).then_inc(win_high, 1)

            def values(step, batch):
                if step.first(1):
                    for b in (B - 2, B - 1):
                        mm.wait_read(act, Step(0, 0), "v", b)
                else:
                    mm.wait_ready(act, Step(step.t, step.v - 1), "pv", C - 1)
                act.dma_start(v_now[:, :], v_all[:, bass.ds(batch, 1), :].rearrange("p a d -> p (a d)"))\
                    .then_inc(v_ready, 16)

            def x_normal(g, t):
                act.wait_ge(x_shift, g.n + 1)
                act.activation(normed[:, t, :], xr[:, g.slot, t, :], ACT.Identity, scale=rstd[:, 0, t:t + 1],
                               bias=shift[:, t:t + 1]).then_inc(x_norm, 1)

            def x_part(step, t):
                tr.wait_ready(act, step, "xT", t)
                act.activation(xT[:, 0, :, P * t:P * (t + 1)], tr.bank(step, "xT", t).rearrange(
                    "p (c r) -> p c r", c=C), ACT.Copy).then_inc(x_high, 1)

            def h_part(step, t):
                tr.wait_ready(act, step, "hT", t)
                act.activation(hT[:, 0, :, P * t:P * (t + 1)], tr.bank(step, "hT", t).rearrange(
                    "p (c r) -> p c r", c=C), ACT.Copy).then_inc(h_high, 1)

            def q_part(step, c):
                mm.wait_ready(act, step, "q", c)
                act.activation(qT[:, step.group(1).parity, 0, c, :], mm.bank(step, "q", c), ACT.Copy)\
                    .then_inc(q_high, 1)

            def exps(step, k):
                g, k, n = half_of(step, k)
                act.wait_ge(shifted, n + 1)
                p = probs[:, g.parity, k // 2, 8 * KEYS * (k % 2):8 * KEYS * (k % 2 + 1)]
                act.activation(p, p, ACT.Exp, scale=DK ** -0.5 / W_SCALE).then_inc(exp_done, 1)

            def p_copies(step, *heads):
                for h in heads:
                    tr.wait_ready(act, step, "pT", h)
                    tr.read(act.activation(pT[0:KEYS, h % 8, :], tr.bank(step, "pT", h)[0:KEYS, :], ACT.Copy),
                            step, "pT", h)

            def a_part(step, c):
                mm.wait_ready(act, step, "pv", c)
                act.activation(aT[:, 0, c, :], mm.bank(step, "pv", c), ACT.Copy).then_inc(a_high, 1)

            def s_part(step):
                mm.wait_ready(act, step, "s", 0)
                act.activation(s_parts[:, :], mm.bank(step, "s", 0), ACT.Identity, bias=bin16[:, 0:1])\
                    .then_inc(s_high, 1)

            def relus(step, *chunks):
                for j in chunks:
                    tr.wait_ready(act, step, "pre", j)
                    tr.read(act.activation(inner[:, j, :], tr.bank(step, "pre", j), ACT.Relu,
                                           bias=inner_cols[:, 1, j:j + 1], scale=w1_div[:, j:j + 1]), step, "pre", j)

            def g_copy(step):
                mm.wait_ready(act, step, "g", 0)
                act.activation(gT[:, 0, :], mm.bank(step, "g", 0), ACT.Identity, bias=b2_col[:, 0:1])\
                    .then_inc(g_high, 1)

            def one_step(step):
                ahead, front, soft, back, ffn = (part in step.parts for part in ALL)
                late = LATE in step.parts
                if step.first(1):
                    ffn_weights()
                if back and step.v % 4 == 1:
                    values(step, step.t + step.v // 4)
                if front:
                    x_normal(step.group(1), 2)
                    x_part(step, 0)
                    x_part(step, 1)
                    x_normal(step.group(1), 3)
                if ffn:
                    s_part(step)
                if back:
                    p_copies(step, 0, 1)
                if ffn:
                    relus(step, 0)
                if back:
                    p_copies(step, 2)
                if ffn:
                    relus(step, 1)
                if back:
                    p_copies(step, 3, 4)
                if ffn:
                    relus(step, 2)
                    relus(step, 3)
                if back:
                    p_copies(step, 5)
                if ffn:
                    relus(step, 4)
                    relus(step, 5)
                if back:
                    exps(step, -1)
                    p_copies(step, 6)
                if ffn:
                    relus(step, 6)
                    relus(step, 7)
                if back:
                    a_part(step, 0)
                    p_copies(step, 7)
                if front:
                    x_part(step, 2)
                if late:
                    wv_copy(step, 0)
                    wv_copy(step, 1)
                    wv_copy(step, 2)
                    wv_copy(step, 3)
                if soft:
                    exps(step, 0)
                if ffn:
                    g_copy(step)
                if back:
                    p_copies(step, 8)
                    a_part(step, 1)
                    p_copies(step, 9, 10, 11)
                if front:
                    x_part(step, 3)
                if late:
                    v_copy(step, 0)
                    v_copy(step, 1)
                if soft:
                    exps(step, 1)
                if back:
                    p_copies(step, 12)
                if soft:
                    exps(step, 2)
                if back:
                    a_part(step, 2)
                    p_copies(step, 13, 14)
                if front:
                    q_part(step, 0)
                if late:
                    v_copy(step, 2)
                    v_copy(step, 3)
                    wo_part(step, 0)
                    wo_part(step, 1)
                if soft:
                    exps(step, 3)
                if back:
                    p_copies(step, 15)
                if soft:
                    exps(step, 4)
                if front:
                    q_part(step, 1)
                if late:
                    wo_part(step, 2)
                    wo_part(step, 3)
                if back:
                    a_part(step, 3)
                if soft:
                    exps(step, 5)
                if front:
                    q_part(step, 2)
                if soft:
                    exps(step, 6)
                if back:
                    h_part(step, 0)
                    h_part(step, 1)
                if front:
                    q_part(step, 3)
                if ahead:
                    x_normal(step.group(2), 0)
                if back:
                    h_part(step, 2)
                    h_part(step, 3)
                if ahead:
                    x_normal(step.group(2), 1)

            run(act, one_step)

        @block.vector
        def _(dve):
            dve.memset(w2_blocks[:, :, :], 0.0).then_inc(zeroed, 1)
            dve.wait_ge(mask_loaded, 16)
            dve.tensor_scalar(mask_bias[:, :, :, :].rearrange("p g t k -> p g (t k)"), mask_raw, 0, MASKED,
                              ALU.is_equal, ALU.mult).then_inc(mask_ready, 1)

            def key_lows():
                for c in range(C):
                    dve.wait_ge(setup_high, c + 1)
                    mm.read(dve.tensor_tensor(
                        kT_all[:, :, 1, c, :], mm.bank(SETUP, "k", c)[:, 0:B * KEYS].rearrange(
                            "p (b k) -> p b k", b=B), kT_all[:, :, 0, c, :], ALU.subtract), SETUP, "k", c)

            def wq_low(c):
                dve.wait_ge(setup_high, C + c + 1)
                tr.read(dve.scalar_tensor_tensor(wqT[:, 1, c, :], tr.bank(SETUP, "wqT", c), W_SCALE, wqT[:, 0, c, :],
                                                 ALU.mult, ALU.subtract), SETUP, "wqT", c)

            def wo_low(step, c):
                dve.wait_ge(setup_high, 2 * C + c + 1)
                tr.read(dve.scalar_tensor_tensor(woT[:, 1, c, :], tr.bank(step, "woT", c), W_SCALE, woT[:, 0, c, :],
                                                 ALU.mult, ALU.subtract), step, "woT", c)

            def ffn_weights():
                dve.wait_ge(wout_high, 1)
                dve.scalar_tensor_tensor(wout_parts[:, 1, :], wout_f, W_SCALE, wout_parts[:, 0, :], ALU.mult,
                                         ALU.subtract).then_inc(wout_low, 1)
                dve.wait_ge(win_high, 1)
                dve.scalar_tensor_tensor(win[:, 1, :, :], win_f[:, :, :, :].rearrange("p c a m -> p c (a m)"), W_SCALE,
                                         win[:, 0, :, :], ALU.mult, ALU.subtract).then_inc(ffn_const, 1)
                dve.wait_ge(ffn_loaded, 16 * (2 * 2 + 2 * J))
                dve.tensor_scalar(bin16[:, :], bin_col[:, :], W_SCALE, None, ALU.mult).then_inc(ffn_const, 1)
                for n in range(2):
                    tr.wait_read(dve, SETUP, "inner", n)
                dve.tensor_scalar(w1_div[:, :], inner_cols[:, 0, :], 1.0 / W_SCALE, None, ALU.mult)\
                    .then_inc(ffn_const, 1)
                dve.wait_ge(pool_const, 10)
                dve.wait_ge(zeroed, 1)
                for j in range(J):
                    first = MJ * (j // 4)
                    twins = w2_blocks[:, j, :].rearrange("p (a m) -> p a m", a=2)[:, :, first:first + MJ]
                    dve.tensor_scalar(twins, units[:, :].unsqueeze(1).broadcast_to([P, 2, MJ]),
                                      inner_cols[:, 2, j:j + 1], None, ALU.mult).then_inc(ffn_const, 1)

            def x_statistics(step, half):
                g = step.group(2)
                dve.wait_ge(x_loaded[g.slot][half], 16 * g.lap + 16)
                for t in (2 * half, 2 * half + 1):
                    dve.bn_stats(stats[:, 0, t, :], xr[:, g.slot, t, :]).then_inc(x_stats, 1)

            def x_means(step):
                for t in range(T):
                    dve.bn_aggr(mean_var[:, 0, t, :], stats[:, 0, t, :]).then_inc(x_mean, 1)
                dve.wait_ge(x_mean, 4 * step.group(2).n + 4)
                dve.tensor_scalar(minus_mean[:, :], mean_var[:, 0, :, 0], -1.0, None, ALU.mult).then_inc(x_minus, 1)
                dve.tensor_scalar(var_eps[:, 0, :], mean_var[:, 0, :, 1], EPS, None, ALU.add).then_inc(x_eps, 1)

            def x_low(step, t):
                dve.wait_ge(x_high, 4 * step.group(1).n + t + 1)
                rows = slice(P * t, P * (t + 1))
                tr.read(dve.tensor_tensor(xT[:, 1, :, rows], tr.bank(step, "xT", t).rearrange("p (c r) -> p c r", c=C),
                                          xT[:, 0, :, rows], ALU.subtract), step, "xT", t)

            def q_low(step, c):
                g = step.group(1)
                dve.wait_ge(q_high, 4 * g.n + c + 1)
                mm.read(dve.tensor_tensor(qT[:, g.parity, 1, c, :], mm.bank(step, "q", c), qT[:, g.parity, 0, c, :],
                                          ALU.subtract), step, "q", c)

            def logits_of(k):
                return lg_banks[:, k % 2, :, 0:LW].rearrange("p b (h k) -> p b h k", k=KEYS)

            def probs_of(g, k):
                return probs[:, g.parity, k // 2, 8 * KEYS * (k % 2):8 * KEYS * (k % 2 + 1)].rearrange(
                    "p (b h k) -> p b h k", b=2, h=HC)

            def maxima(step, k):
                g, k, n = half_of(step, k)
                dve.wait_ge(lg_ready, n + 1)
                if step.first(0) and k == 0:
                    dve.wait_ge(mask_ready, 1)
                dve.tensor_tensor(probs_of(g, k), logits_of(k),
                                  mask_bias[:, g.slot, k // 2, :].unsqueeze(1).unsqueeze(1).broadcast_to(
                                      [P, 2, HC, KEYS]), ALU.add).then_inc(lg_free, 1)
                dve.wait_ge(lg_free, n + 1)
                dve.tensor_reduce(row_max[:, g.parity, k, :, :], probs_of(g, k), AX.X, ALU.max)\
                    .then_inc(max_done, 1)

            def sums(step, k):
                g, k, n = half_of(step, k)
                p = probs[:, g.parity, k // 2, 8 * KEYS * (k % 2):8 * KEYS * (k % 2 + 1)].rearrange(
                    "p (b h k) -> p b h k", b=2, h=HC)
                dve.wait_ge(exp_done, n + 1)
                dve.tensor_reduce(row_sum[:, k % 2, :, :], p, AX.X, ALU.add).then_inc(sum_done, 1)
                dve.wait_ge(sum_done, n + 1)
                dve.reciprocal(row_inv[:, g.parity, k, :, :], row_sum[:, k % 2, :, :]).then_inc(inv_done, 1)

            def a_low(step, c):
                dve.wait_ge(a_high, 4 * step.group(-1).n + c + 1)
                mm.read(dve.tensor_tensor(aT[:, 1, c, :], mm.bank(step, "pv", c), aT[:, 0, c, :], ALU.subtract),
                        step, "pv", c)

            def residual(step, t):
                g = step.group(-1)
                h = xr[:, g.slot, t, :]
                mm.wait_ready(dve, step, "wo", t)
                mm.read(dve.scalar_tensor_tensor(h, mm.bank(step, "wo", t), 1.0 / W_SCALE, h, ALU.mult, ALU.add),
                        step, "wo", t)
                mm.wait_read(dve, step, "wo", t)
                dve.bn_stats(stats[:, 1, t, :], h).then_inc(h_stats, 1)

            def h_means(step, pair):
                for t in (2 * pair, 2 * pair + 1):
                    dve.bn_aggr(mean_var[:, 1, t, :], stats[:, 1, t, :]).then_inc(h_mean, 1)
                dve.wait_ge(h_mean, 4 * step.group(-1).n + 2 * pair + 2)
                tiles = slice(2 * pair, 2 * pair + 2)
                dve.tensor_scalar(var_eps[:, 1, tiles], mean_var[:, 1, tiles, 1], EPS, None, ALU.add).then_inc(h_eps, 1)

            def h_normal(step, t):
                g = step.group(-1)
                dve.wait_ge(h_rstd, 2 * g.n + t // 2 + 1)
                dve.tensor_scalar(normed[:, t, :], xr[:, g.slot, t, :], mean_var[:, 1, t, 0:1], rstd[:, 1, t:t + 1],
                                  ALU.subtract, ALU.mult).then_inc(h_norm, 1)

            def h_low(step, t):
                dve.wait_ge(h_high, 4 * step.group(-1).n + t + 1)
                rows = slice(P * t, P * (t + 1))
                tr.read(dve.tensor_tensor(hT[:, 1, :, rows], tr.bank(step, "hT", t).rearrange("p (c r) -> p c r", c=C),
                                          hT[:, 0, :, rows], ALU.subtract), step, "hT", t)

            def s_low(step):
                dve.wait_ge(s_high, step.group(-2).n + 1)
                low = s_parts[M:2 * M, :]
                mm.read(dve.scalar_tensor_tensor(low, mm.bank(step, "s", 0)[M:2 * M, :], bin16[M:2 * M, 0:1], low,
                                                 ALU.add, ALU.subtract), step, "s", 0)

            def g_low(step):
                dve.wait_ge(g_high, step.group(-2).n + 1)
                mm.read(dve.scalar_tensor_tensor(gT[:, 1, :], mm.bank(step, "g", 0), b2_col[:, 0:1], gT[:, 0, :],
                                                 ALU.add, ALU.subtract), step, "g", 0)

            def output(step, t):
                h = xr[:, step.group(-2).slot, t, :]
                dve.wait_ge(bout_added, 4 * step.group(-2).n + t + 1)
                mm.wait_ready(dve, step, "out", t)
                mm.read(dve.scalar_tensor_tensor(h, mm.bank(step, "out", t), 1.0 / W_SCALE, h, ALU.mult, ALU.add),
                        step, "out", t)

            def one_step(step):
                ahead, front, soft, back, ffn = (part in step.parts for part in ALL)
                late = LATE in step.parts
                if step.first(-1):
                    key_lows()
                    for c in range(C):
                        wq_low(c)
                if step.first(1):
                    ffn_weights()
                if back:
                    maxima(step, -1)
                if front:
                    x_low(step, 0)
                    x_low(step, 1)
                if ffn:
                    s_low(step)
                if soft:
                    maxima(step, 0)
                    maxima(step, 1)
                    maxima(step, 2)
                    maxima(step, 3)
                if back:
                    sums(step, -1)
                if soft:
                    maxima(step, 4)
                if back:
                    a_low(step, 0)
                if front:
                    x_low(step, 2)
                if soft:
                    sums(step, 0)
                if ffn:
                    g_low(step)
                if back:
                    a_low(step, 1)
                if ffn:
                    output(step, 0)
                    output(step, 1)
                    output(step, 2)
                if front:
                    x_low(step, 3)
                if ffn:
                    output(step, 3)
                if soft:
                    sums(step, 1)
                    maxima(step, 5)
                if back:
                    a_low(step, 2)
                if front:
                    q_low(step, 0)
                if late:
                    wo_low(step, 0)
                    wo_low(step, 1)
                if soft:
                    sums(step, 2)
                    sums(step, 3)
                if front:
                    q_low(step, 1)
                if late:
                    wo_low(step, 2)
                    wo_low(step, 3)
                if back:
                    a_low(step, 3)
                if soft:
                    maxima(step, 6)
                if ahead:
                    x_statistics(step, 0)
                if front:
                    q_low(step, 2)
                if ahead:
                    x_statistics(step, 1)
                    dve.wait_ge(x_stats, 4 * step.group(2).n + 4)
                if soft:
                    sums(step, 4)
                if ahead:
                    x_means(step)
                if back:
                    residual(step, 0)
                    residual(step, 1)
                    dve.wait_ge(h_stats, 4 * step.group(-1).n + 2)
                if soft:
                    sums(step, 5)
                if back:
                    h_means(step, 0)
                    residual(step, 2)
                    h_normal(step, 0)
                    h_normal(step, 1)
                    residual(step, 3)
                    dve.wait_ge(h_stats, 4 * step.group(-1).n + 4)
                    h_low(step, 0)
                    h_means(step, 1)
                    h_low(step, 1)
                    h_normal(step, 2)
                    h_normal(step, 3)
                if front:
                    q_low(step, 3)
                if back:
                    h_low(step, 2)
                    h_low(step, 3)
                if soft:
                    sums(step, 6)

            run(dve, one_step)

        @block.tensor
        def _(pe):
            pe.wait_ge(pool_const, 2)

            pe.wait_ge(ctx_loaded, 16)
            for c in range(C):
                tr.wait_free(pe, SETUP, "ctxT", c)
                bank = tr.bank(SETUP, "ctxT", c)
                for b in range(B):
                    last = pe.transpose(bank[:, KEYS * b:KEYS * (b + 1)], ctx_raw[:, b, P * c:P * (c + 1)],
                                        ident[0:KEYS, 0:KEYS])
                last.then_inc(tr_ready, 1)

            pe.wait_ge(rows_loaded, 48)
            for n in range(2):
                tr.wait_free(pe, SETUP, "inner", n)
                size = (2 - n) * J
                pe.transpose(tr.bank(SETUP, "inner", n)[:, 0:size], in_rows[n], ident[0:size, 0:size])\
                    .then_inc(tr_ready, 1)

            def weight(step, n, name, *chunks):
                for c in chunks:
                    if c == 0:
                        pe.wait_ge(w_loaded[n], 16)
                    tr.wait_free(pe, step, name, c)
                    bank = tr.bank(step, name, c)
                    for o in range(C):
                        last = pe.transpose(bank[:, P * o:P * (o + 1)], w_raw[n][:, o, P * c:P * (c + 1)], ident[:, :])
                    last.then_inc(tr_ready, 1)

            weight(SETUP, 0, "wkT", *range(C))
            for c in range(C):
                tr.wait_read(pe, SETUP, "wkT", c)
            for o in range(C):
                mm.wait_free(pe, SETUP, "k", o)
                for c in range(C):
                    last = pe.matmul(mm.bank(SETUP, "k", o)[:, 0:B * KEYS], wkT[:, c, P * o:P * (o + 1)],
                                     ctxT[:, c, :], start=(c == 0), stop=(c == C - 1))
                last.then_inc(mm_ready, 1)
            weight(SETUP, 1, "wqT", *range(C))

            def values(step, b):
                if b == 0:
                    for c in range(C):
                        tr.wait_read(pe, step, "wvT", c)
                mm.wait_free(pe, step, "v", b)
                for c in range(C):
                    last = pe.matmul(mm.bank(step, "v", b)[0:KEYS, :], ctxT[:, c, KEYS * b:KEYS * (b + 1)],
                                     wvT[:, c, :], start=(c == 0), stop=(c == C - 1))
                last.then_inc(mm_ready, 1)

            def three_passes(bank, stationary, moving, chunks):
                passes = [(c, a, b) for c in range(chunks) for a, b in ((0, 0), (0, 1), (1, 0))]
                for n, (c, a, b) in enumerate(passes):
                    last = pe.matmul(bank, stationary(a, c), moving(b, c), start=(n == 0),
                                     stop=(n == len(passes) - 1))
                return last

            def x_transpose(step, t):
                g = step.group(1)
                tr.wait_free(pe, step, "xT", t)
                pe.wait_ge(x_norm, 4 * g.n + t + 1)
                for c in range(C):
                    last = pe.transpose(tr.bank(step, "xT", t)[:, P * c:P * (c + 1)], normed[:, t, P * c:P * (c + 1)],
                                        ident[:, :])
                last.then_inc(tr_ready, 1)

            def q(step, o):
                if o == 0:
                    for t in (T - 2, T - 1):
                        tr.wait_read(pe, step, "xT", t)
                    if step.first(-1):
                        for c in (C - 2, C - 1):
                            tr.wait_read(pe, SETUP, "wqT", c)
                mm.wait_free(pe, step, "q", o)
                three_passes(mm.bank(step, "q", o), lambda a, c: wqT[:, a, c, P * o:P * (o + 1)],
                             lambda b, c: xT[:, b, c, :], C).then_inc(mm_ready, 1)

            def logits(step, k):
                n = HALVES * step.i + k
                g = step.group(0)
                t, u = k // 2, k % 2
                if k == 0:
                    mm.wait_all_read(pe, step)
                buffer = step.v % 4 // 2
                if k == 0 and step.v % 2 == 0:
                    pe.wait_ge(k_ready[buffer], 16 * HC * (step.t + step.v // 4 + 1))
                if not (isinstance(n, int) and n < 2):
                    pe.wait_ge(lg_free, n - 1)
                rows = slice(P * t, P * (t + 1))
                for b in range(2):
                    c = 2 * u + b
                    bank = lg_banks[:, k % 2, b, 0:LW]
                    for m, (qp, kp) in enumerate(((0, 0), (0, 1), (1, 0))):
                        last = pe.matmul(bank, qT[:, g.parity, qp, c, rows], k_blocks[:, buffer, kp, c, :],
                                         start=(m == 0), stop=(m == 2))
                last.then_inc(lg_ready, 1)

            def p_transposes(step, *heads):
                g = step.group(-1)
                if 0 in heads or HEADS // 2 in heads:
                    pe.wait_ge(probs_ready, HALVES * g.n + HALVES - (0 in heads))
                for h in heads:
                    tr.wait_free(pe, step, "pT", h)
                    for t in range(T):
                        last = pe.transpose(tr.bank(step, "pT", h)[0:KEYS, P * t:P * (t + 1)],
                                            probs[:, g.parity, t, KEYS * h:KEYS * (h + 1)], ident[:, :])
                    last.then_inc(tr_ready, 1)

            def pv(step, c):
                if c == 0 and step.v % 4 == 1:
                    pe.wait_ge(v_ready, 16 * (step.t + step.v // 4 + 1))
                for h in (2, 3):
                    tr.wait_read(pe, step, "pT", HC * c + h)
                mm.wait_free(pe, step, "pv", c)
                for h in range(HC):
                    last = pe.matmul(mm.bank(step, "pv", c)[DK * h:DK * (h + 1), :],
                                     v_now[:, DK * (HC * c + h):DK * (HC * c + h + 1)], pT[0:KEYS, (HC * c + h) % 8, :],
                                     start=True, stop=True)
                last.then_inc(mm_ready, 1)

            def wo(step, t):
                if t == 0:
                    for c in (C - 2, C - 1):
                        mm.wait_read(pe, step, "pv", c)
                    if step.first(1):
                        for c in (C - 2, C - 1):
                            tr.wait_read(pe, Step(0, 0), "woT", c)
                mm.wait_free(pe, step, "wo", t)
                three_passes(mm.bank(step, "wo", t), lambda a, c: aT[:, a, c, P * t:P * (t + 1)],
                             lambda b, c: woT[:, b, c, :], C).then_inc(mm_ready, 1)

            def h_transpose(step, t):
                tr.wait_free(pe, step, "hT", t)
                pe.wait_ge(h_norm, 4 * step.group(-1).n + t + 1)
                for c in range(C):
                    last = pe.transpose(tr.bank(step, "hT", t)[:, P * c:P * (c + 1)], normed[:, t, P * c:P * (c + 1)],
                                        ident[:, :])
                last.then_inc(tr_ready, 1)

            def ffn_in(step):
                tr.wait_all_read(pe, step)
                mm.wait_free(pe, step, "s", 0)
                three_passes(mm.bank(step, "s", 0), lambda a, c: win[:, a, c, :], lambda b, c: hT[:, b, c, :], C)\
                    .then_inc(mm_ready, 1)

            def ffn_pre(step, j):
                if j == 0:
                    mm.wait_read(pe, step, "s", 0)
                tr.wait_free(pe, step, "pre", j)
                pe.matmul(tr.bank(step, "pre", j), spread[:, j, :], s_parts[:, :], start=True, stop=True)\
                    .then_inc(tr_ready, 1)

            def ffn_g(step, j):
                if j == 0:
                    mm.wait_free(pe, step, "g", 0)
                tr.wait_read(pe, step, "pre", j)
                group = DK * (j % 4)
                last = pe.matmul(mm.bank(step, "g", 0)[group:group + DK, :], w2_blocks[:, j, :], inner[:, j, :],
                                 start=(j < 4), stop=(j >= 4))
                if j == J - 1:
                    last.then_inc(mm_ready, 1)

            def ffn_out(step, t):
                if t == 0:
                    mm.wait_read(pe, step, "g", 0)
                mm.wait_free(pe, step, "out", t)
                for part in range(2):
                    last = pe.matmul(mm.bank(step, "out", t), gT[:, part, P * t:P * (t + 1)], wout[:, :],
                                     start=(part == 0), stop=(part == 1))
                last.then_inc(mm_ready, 1)

            def one_step(step):
                ahead, front, soft, back, ffn = (part in step.parts for part in ALL)
                late = LATE in step.parts
                if soft:
                    logits(step, 0)
                if front:
                    x_transpose(step, 0)
                    x_transpose(step, 1)
                if ffn:
                    ffn_in(step)
                if back:
                    p_transposes(step, 0, 1)
                if soft:
                    logits(step, 1)
                if ffn:
                    ffn_pre(step, 0)
                if back:
                    p_transposes(step, 2)
                if soft:
                    logits(step, 2)
                if ffn:
                    ffn_pre(step, 1)
                if back:
                    p_transposes(step, 3, 4)
                if ffn:
                    ffn_pre(step, 2)
                if soft:
                    logits(step, 3)
                if ffn:
                    ffn_pre(step, 3)
                if back:
                    p_transposes(step, 5)
                if ffn:
                    ffn_pre(step, 4)
                    ffn_pre(step, 5)
                if back:
                    pv(step, 0)
                    p_transposes(step, 6)
                if ffn:
                    ffn_pre(step, 6)
                if soft:
                    logits(step, 4)
                if ffn:
                    ffn_pre(step, 7)
                if soft:
                    logits(step, 5)
                if back:
                    p_transposes(step, 7)
                if front:
                    x_transpose(step, 2)
                if late:
                    weight(step, 2, "wvT", 0, 1, 2, 3)
                if ffn:
                    for j in range(J):
                        ffn_g(step, j)
                if back:
                    p_transposes(step, 8)
                    pv(step, 1)
                    p_transposes(step, 9)
                if ffn:
                    ffn_out(step, 0)
                if back:
                    p_transposes(step, 10, 11)
                if ffn:
                    ffn_out(step, 1)
                    ffn_out(step, 2)
                if front:
                    x_transpose(step, 3)
                if late:
                    values(step, 0)
                    values(step, 1)
                if back:
                    p_transposes(step, 12)
                if ffn:
                    ffn_out(step, 3)
                if back:
                    pv(step, 2)
                    p_transposes(step, 13, 14)
                if front:
                    q(step, 0)
                if late:
                    values(step, 2)
                    values(step, 3)
                    weight(step, 3, "woT", 0, 1)
                if back:
                    p_transposes(step, 15)
                if front:
                    q(step, 1)
                if late:
                    weight(step, 3, "woT", 2, 3)
                if back:
                    pv(step, 3)
                if soft:
                    logits(step, 6)
                if front:
                    q(step, 2)
                if back:
                    wo(step, 0)
                    wo(step, 1)
                    wo(step, 2)
                    wo(step, 3)
                    h_transpose(step, 0)
                    h_transpose(step, 1)
                if front:
                    q(step, 3)
                if soft:
                    logits(step, 7)
                if back:
                    h_transpose(step, 2)
                    h_transpose(step, 3)
                if step.first(FIRST_FULL - 1):
                    pe.wait_ge(ffn_const, 3 + J)
                    pe.wait_ge(wout_placed, 2 * 16 * J)
                    pe.wait_ge(pool_const, 10)

            run(pe, one_step)


_INS = ['x', 'ctx_1024', 'mask_1x1xSxS2_ik0', 'L0_xattn_Wq', 'L0_xattn_Wk', 'L0_xattn_Wv', 'L0_xattn_Wo',
        'L0_ffn_Win', 'L0_ffn_bin_', 'L0_ffn_W1', 'L0_ffn_b1', 'L0_ffn_W2', 'L0_ffn_b2', 'L0_ffn_Wout', 'L0_ffn_bout']


def kernel(**inputs):
    import numpy as _np
    import concourse.bacc as _bacc
    from concourse import mybir as _mybir
    from concourse.bass_utils import run_bass_kernel_spmd as _run

    nc = _bacc.Bacc("TRN2", target_bir_lowering=False, num_devices=1)
    arrays, args = {}, []
    for name in _INS:
        a = _np.ascontiguousarray(inputs[name])
        arrays[f"in_{name}"] = a
        args.append(nc.dram_tensor(f"in_{name}", a.shape, _mybir.dt.from_np(a.dtype), kind="ExternalInput").ap())
    args.append(nc.dram_tensor("out_x", (B, S, D), _mybir.dt.float32, kind="ExternalOutput").ap())
    build(nc, *args)
    r = _run(nc, [arrays], core_ids=[0])
    return r.results[0]["out_x"]
```
